# Optimizing a Trainium2 kernel written in Bass

```python
import numpy as np
import jax
import jax.numpy as jnp

def _softmax(x, axis=-1):
    return jax.nn.softmax(x, axis=axis)

def _gelu(x):
    return jax.nn.gelu(x, approximate=True)

def _silu(x):
    return jax.nn.silu(x)

def _sigmoid(x):
    return jax.nn.sigmoid(x)

def _layernorm(x, axis=-1, eps=1e-05):
    m = jnp.mean(x, axis=axis, keepdims=True)
    v = jnp.var(x, axis=axis, keepdims=True)
    return (x - m) / jnp.sqrt(v + eps)

def _scatter_add(tgt, idx, src, axis=0):
    return tgt.at[idx].add(src)

def _segment_sum(src, seg, n):
    return jax.ops.segment_sum(src, seg, n)
kernel_name = 'mk_flamingo_gated_d1_seqx_r8_f0afee'

def setup_inputs(seed: int=0):
    np.random.seed(seed)
    _w = jnp.asarray

    def _rec_inputs():
        import jax
        import jax.numpy as jnp
        _rk = jax.random.key(seed)
        x = 4.136e-05 + 0.9999 * jax.random.normal(jax.random.fold_in(_rk, 1), (4, 256, 256), jnp.float32)
        _lenS = 256 - jax.random.randint(jax.random.fold_in(_rk, 7), (4,), 0, max(1, 256 // 4) + 1, jnp.int32)
        _lenS2 = 256 - jax.random.randint(jax.random.fold_in(_rk, 8), (4,), 0, max(1, 256 // 4) + 1, jnp.int32)
        _ctx_1024P = jax.random.normal(jax.random.fold_in(_rk, 11), (4, 16, 128), jnp.float32)
        _ctx_1024c = jax.random.dirichlet(jax.random.fold_in(_rk, 511), 0.3 * jnp.ones((16,), jnp.float32), (4, 256))
        _ctx_1024t = jnp.einsum('bsk,bkd->bsd', _ctx_1024c, _ctx_1024P)
        _ctx_1024t = _ctx_1024t * jax.lax.rsqrt(jnp.mean(jnp.square(_ctx_1024t)) + 1e-12) * 0.953939
        ctx_1024 = -0.000292821 + 1.00034 * (_ctx_1024t + 0.3 * jax.random.normal(jax.random.fold_in(_rk, 611), (4, 256, 128), jnp.float32))
        _g = jax.random.normal(jax.random.fold_in(_rk, 9001), (2, 1), jnp.float32)
        _g = jnp.sign(_g) * jnp.maximum(jnp.abs(_g), 1.0) + (_g == 0) * 1.0
        g_xattn = _g[0]
        g_ffn = _g[1]
        return (x, ctx_1024, g_xattn, g_ffn)
    x, ctx_1024, g_xattn, g_ffn = _rec_inputs()

    def _L0_xattn_setup():
        import jax, jax.numpy as jnp
        import numpy as np
        import math
        B, L, DM = (2, 256, 128)
        DS, DC, EXP = (16, 4, 2)
        DI = EXP * DM
        DR = math.ceil(DM / 16)
        DT_MIN, DT_MAX, DT_FLOOR = (0.001, 0.1, 0.0001)

        def _ssm_forward(hidden_states, z, in_proj_w, conv_w, conv_b, x_proj_w, dt_proj_w, dt_proj_b, A_log, D):
            b = hidden_states.shape[0]
            x = jnp.einsum('ed,bld->bel', in_proj_w, hidden_states)
            xp = jnp.pad(x, ((0, 0), (0, 0), (DC - 1, 0)))
            xc = jax.lax.conv_general_dilated(xp, conv_w[:, None, :], window_strides=(1,), padding='VALID', dimension_numbers=('NCH', 'OIH', 'NCH'), feature_group_count=DI)
            u = jax.nn.silu(xc + conv_b[None, :, None])
            x_dbl = jnp.einsum('ke,bel->bkl', x_proj_w, u)
            dt_lo = x_dbl[:, :DR]
            Bm = x_dbl[:, DR:DR + DS]
            Cm = x_dbl[:, DR + DS:]
            delta = jax.nn.softplus(jnp.einsum('er,brl->bel', dt_proj_w, dt_lo) + dt_proj_b[None, :, None])
            A = -jnp.exp(A_log)

            def step(state, xs):
                d_t, B_t, C_t, u_t = xs
                dA = jnp.exp(d_t[..., None] * A)
                state = state * dA + (d_t * u_t)[..., None] * B_t[:, None, :]
                y_t = jnp.einsum('ben,bn->be', state, C_t)
                return (state, y_t)
            xs = (jnp.moveaxis(delta, -1, 0), jnp.moveaxis(Bm, -1, 0), jnp.moveaxis(Cm, -1, 0), jnp.moveaxis(u, -1, 0))
            state0 = jnp.zeros((b, DI, DS), delta.dtype)
            _, ys = jax.lax.scan(step, state0, xs)
            y = jnp.moveaxis(ys, 0, -1)
            y = y + D[None, :, None] * u
            y = y * jax.nn.silu(z)
            return jnp.swapaxes(y, 1, 2)
        key = jax.random.key(seed)
        ks = jax.random.split(key, 8)
        hidden_states = jax.random.normal(ks[0], (B, L, DM), jnp.float32)
        z = jax.random.normal(ks[1], (B, DI, L), jnp.float32)
        in_proj_w = jax.random.normal(ks[2], (DI, DM), jnp.float32) * DM ** (-0.5)
        conv_w = jax.random.normal(ks[3], (DI, DC), jnp.float32) * DC ** (-0.5)
        conv_b = jnp.zeros((DI,), jnp.float32)
        x_proj_w = jax.random.normal(ks[4], (DR + 2 * DS, DI), jnp.float32) * DI ** (-0.5)
        dt_std = DR ** (-0.5)
        dt_proj_w = jax.random.uniform(ks[5], (DI, DR), jnp.float32, -dt_std, dt_std)
        dt = jnp.exp(jax.random.uniform(ks[6], (DI,), jnp.float32) * (math.log(DT_MAX) - math.log(DT_MIN)) + math.log(DT_MIN))
        dt = jnp.clip(dt, DT_FLOOR)
        dt_proj_b = dt + jnp.log(-jnp.expm1(-dt))
        A_log = jnp.log(jnp.broadcast_to(jnp.arange(1, DS + 1, dtype=jnp.float32), (DI, DS)))
        D = jnp.ones((DI,), jnp.float32)
        return dict(hidden_states=hidden_states, z=z, in_proj_w=in_proj_w, conv_w=conv_w, conv_b=conv_b, x_proj_w=x_proj_w, dt_proj_w=dt_proj_w, dt_proj_b=dt_proj_b, A_log=A_log, D=D)
    _L0_xattn_all = _L0_xattn_setup()
    _L0_xattn_in = {k: v for k, v in _L0_xattn_all.items() if k in ('in_proj_w', 'conv_w', 'conv_b', 'x_proj_w', 'dt_proj_w', 'dt_proj_b', 'A_log', 'D')}
    del _L0_xattn_all

    def _L0_ffn_setup():
        import jax, jax.numpy as jnp
        import numpy as np
        ACT_BITS = 8
        EPS = 1e-05

        def act_quant(x, bits=ACT_BITS):
            qb = float(2 ** (bits - 1))
            scale = qb / jnp.clip(jnp.max(jnp.abs(x), axis=-1, keepdims=True), EPS)
            xq = jnp.clip(jnp.round(x * scale), -qb, qb - 1) / scale
            return x + jax.lax.stop_gradient(xq - x)

        def weight_quant(w):
            scale = 1.0 / jnp.clip(jnp.mean(jnp.abs(w)), EPS)
            wq = jnp.clip(jnp.round(w * scale), -1.0, 1.0) / scale
            return w + jax.lax.stop_gradient(wq - w)

        def fwht(x):
            shape = x.shape
            n = shape[-1]
            x = x.reshape(-1, n)
            h = 1
            while h < n:
                x = x.reshape(-1, n // (2 * h), 2, h)
                a, b = (x[..., 0, :], x[..., 1, :])
                x = jnp.stack([a + b, a - b], axis=-2).reshape(-1, n)
                h *= 2
            return (x * (1.0 / np.sqrt(n)).astype(np.float32)).reshape(shape)

        def bitlinear(x, w):
            return jnp.einsum('bsh,oh->bso', act_quant(x), weight_quant(w))

        def h_bitlinear(x, w):
            return jnp.einsum('bsh,oh->bso', act_quant(fwht(x)), weight_quant(w))
        key = jax.random.key(seed)
        k1, k2, k3, k4 = jax.random.split(key, 4)
        H, I = (256, 1024)
        B, S = (4, 256)
        std_in = 1.0 / np.sqrt(H)
        std_mid = 1.0 / np.sqrt(I)
        return {'x': jax.random.normal(k1, (B, S, H), dtype=jnp.float32), 'w_gate': jax.random.normal(k2, (I, H), dtype=jnp.float32) * std_in, 'w_up': jax.random.normal(k3, (I, H), dtype=jnp.float32) * std_in, 'w_down': jax.random.normal(k4, (H, I), dtype=jnp.float32) * std_mid}
    _L0_ffn_all = _L0_ffn_setup()
    _L0_ffn_in = {k: v for k, v in _L0_ffn_all.items() if k in ('w_gate', 'w_up', 'w_down')}
    del _L0_ffn_all
    return {'x': x, 'ctx_1024': ctx_1024, 'g_xattn': g_xattn, 'g_ffn': g_ffn, 'L0_xattn_in_proj_w': _L0_xattn_in['in_proj_w'], 'L0_xattn_conv_w': _L0_xattn_in['conv_w'], 'L0_xattn_conv_b': _L0_xattn_in['conv_b'], 'L0_xattn_x_proj_w': _L0_xattn_in['x_proj_w'], 'L0_xattn_dt_proj_w': _L0_xattn_in['dt_proj_w'], 'L0_xattn_dt_proj_b': _L0_xattn_in['dt_proj_b'], 'L0_xattn_A_log': _L0_xattn_in['A_log'], 'L0_xattn_D': _L0_xattn_in['D'], 'L0_ffn_w_gate': _L0_ffn_in['w_gate'], 'L0_ffn_w_up': _L0_ffn_in['w_up'], 'L0_ffn_w_down': _L0_ffn_in['w_down']}

def reference(x, ctx_1024, g_xattn, g_ffn, L0_xattn_in_proj_w, L0_xattn_conv_w, L0_xattn_conv_b, L0_xattn_x_proj_w, L0_xattn_dt_proj_w, L0_xattn_dt_proj_b, L0_xattn_A_log, L0_xattn_D, L0_ffn_w_gate, L0_ffn_w_up, L0_ffn_w_down):
    import jax
    import jax.numpy as jnp

    def _L0_xattn_ref(hidden_states, z, in_proj_w, conv_w, conv_b, x_proj_w, dt_proj_w, dt_proj_b, A_log, D):
        import jax, jax.numpy as jnp
        import numpy as np
        import math
        B, L, DM = (2, 256, 128)
        DS, DC, EXP = (16, 4, 2)
        DI = EXP * DM
        DR = math.ceil(DM / 16)
        DT_MIN, DT_MAX, DT_FLOOR = (0.001, 0.1, 0.0001)

        def _ssm_forward(hidden_states, z, in_proj_w, conv_w, conv_b, x_proj_w, dt_proj_w, dt_proj_b, A_log, D):
            b = hidden_states.shape[0]
            x = jnp.einsum('ed,bld->bel', in_proj_w, hidden_states)
            xp = jnp.pad(x, ((0, 0), (0, 0), (DC - 1, 0)))
            xc = jax.lax.conv_general_dilated(xp, conv_w[:, None, :], window_strides=(1,), padding='VALID', dimension_numbers=('NCH', 'OIH', 'NCH'), feature_group_count=DI)
            u = jax.nn.silu(xc + conv_b[None, :, None])
            x_dbl = jnp.einsum('ke,bel->bkl', x_proj_w, u)
            dt_lo = x_dbl[:, :DR]
            Bm = x_dbl[:, DR:DR + DS]
            Cm = x_dbl[:, DR + DS:]
            delta = jax.nn.softplus(jnp.einsum('er,brl->bel', dt_proj_w, dt_lo) + dt_proj_b[None, :, None])
            A = -jnp.exp(A_log)

            def step(state, xs):
                d_t, B_t, C_t, u_t = xs
                dA = jnp.exp(d_t[..., None] * A)
                state = state * dA + (d_t * u_t)[..., None] * B_t[:, None, :]
                y_t = jnp.einsum('ben,bn->be', state, C_t)
                return (state, y_t)
            xs = (jnp.moveaxis(delta, -1, 0), jnp.moveaxis(Bm, -1, 0), jnp.moveaxis(Cm, -1, 0), jnp.moveaxis(u, -1, 0))
            state0 = jnp.zeros((b, DI, DS), delta.dtype)
            _, ys = jax.lax.scan(step, state0, xs)
            y = jnp.moveaxis(ys, 0, -1)
            y = y + D[None, :, None] * u
            y = y * jax.nn.silu(z)
            return jnp.swapaxes(y, 1, 2)
        return _ssm_forward(hidden_states, z, in_proj_w, conv_w, conv_b, x_proj_w, dt_proj_w, dt_proj_b, A_log, D)

    def _L0_ffn_ref(x, w_gate, w_up, w_down):
        import jax, jax.numpy as jnp
        import numpy as np
        ACT_BITS = 8
        EPS = 1e-05

        def act_quant(x, bits=ACT_BITS):
            qb = float(2 ** (bits - 1))
            scale = qb / jnp.clip(jnp.max(jnp.abs(x), axis=-1, keepdims=True), EPS)
            xq = jnp.clip(jnp.round(x * scale), -qb, qb - 1) / scale
            return x + jax.lax.stop_gradient(xq - x)

        def weight_quant(w):
            scale = 1.0 / jnp.clip(jnp.mean(jnp.abs(w)), EPS)
            wq = jnp.clip(jnp.round(w * scale), -1.0, 1.0) / scale
            return w + jax.lax.stop_gradient(wq - w)

        def fwht(x):
            shape = x.shape
            n = shape[-1]
            x = x.reshape(-1, n)
            h = 1
            while h < n:
                x = x.reshape(-1, n // (2 * h), 2, h)
                a, b = (x[..., 0, :], x[..., 1, :])
                x = jnp.stack([a + b, a - b], axis=-2).reshape(-1, n)
                h *= 2
            return (x * (1.0 / np.sqrt(n)).astype(np.float32)).reshape(shape)

        def bitlinear(x, w):
            return jnp.einsum('bsh,oh->bso', act_quant(x), weight_quant(w))

        def h_bitlinear(x, w):
            return jnp.einsum('bsh,oh->bso', act_quant(fwht(x)), weight_quant(w))
        gate = bitlinear(x, w_gate)
        up = bitlinear(x, w_up)
        intermediate = jax.nn.silu(gate) * up
        return h_bitlinear(intermediate, w_down)
    x = x + jnp.tanh(g_xattn[0]) * _L0_xattn_ref(ctx_1024, _layernorm(x, axis=-1), L0_xattn_in_proj_w, L0_xattn_conv_w, L0_xattn_conv_b, L0_xattn_x_proj_w, L0_xattn_dt_proj_w, L0_xattn_dt_proj_b, L0_xattn_A_log, L0_xattn_D)
    x = x + jnp.tanh(g_ffn[0]) * _L0_ffn_ref(_layernorm(x, axis=-1), L0_ffn_w_gate, L0_ffn_w_up, L0_ffn_w_down)
    return x

_drawn_inputs = setup_inputs


def setup_inputs(seed=0):
    import zlib

    import numpy as np

    out = dict(_drawn_inputs(seed))
    spreads = {'L0_xattn_conv_b': (0.0, 0.1), 'L0_xattn_D': (1.0, 0.2)}
    factors = {}
    for name, (base, spread) in spreads.items():
        noise = np.random.default_rng([zlib.crc32(name.encode()), seed]).standard_normal(out[name].shape)
        drawn = base * np.exp(spread * noise) if base else spread * noise
        out[name] = jnp.asarray(drawn.astype(out[name].dtype))
    for name, factor in factors.items():
        out[name] = (out[name] * factor).astype(out[name].dtype)
    return out
```

```python
import math
from contextlib import ExitStack

import concourse.bass as bass
from concourse import mybir

F32 = mybir.dt.float32
BF16 = mybir.dt.bfloat16
ALU = mybir.AluOpType
ACT = mybir.ActivationFunctionType
AX = mybir.AxisListType

P = 128
B, L, E = 4, 256, 256
DM, DS, DR, DC = 128, 16, 8, 4
I = 1024
HALF = E // P
LC = L // P
NI = I // P
NB = 2
STEPS = DS // NB
AHEAD = 3
RING = 4
STATES = 3
LN_EPS = 1e-5
Q_EPS = 1e-5
QB = 128.0
MAGIC = 1.5 * 2.0 ** 23
DT0 = 96


class Chain:

    def __init__(self, sem, per_batch):
        self.sem, self.per_batch = sem, per_batch

    def begin(self, eng, batch):
        self.eng, self.base, self.count = eng, batch * self.per_batch, 0
        return self

    def __call__(self, ins):
        self.count += 1
        ins.then_inc(self.sem, 1)
        self.eng.wait_ge(self.sem, self.base + self.count)

    def end(self):
        assert self.count == self.per_batch, (self.count, self.per_batch)


def gated_ssm_ffn(nc, x, ctx_1024, g_xattn, g_ffn, in_proj_w, conv_w, conv_b, x_proj_w, dt_proj_w, dt_proj_b,
                  A_log, D, w_gate, w_up, w_down, ident, hadamard, out):
    stack = ExitStack()
    with stack:
        def sb(name, shape, dt=F32):
            return stack.enter_context(nc.sbuf_tensor(name, shape, dt))

        def sem(name):
            return stack.enter_context(nc.semaphore(name))

        xs = sb("xs", [P, B, LC, E])
        ctxs = sb("ctxs", [P, B, LC, DM])
        ctxT = sb("ctxT", [DM, B, L])
        id32 = sb("id32", [P, P])
        id16 = sb("id16", [P, P], BF16)
        had = sb("had", [P, P])
        sel = sb("sel", [3 * 2 * DS, 2 * DS], BF16)
        inw = sb("inw", [P, HALF, DM])
        inwk = sb("inwk", [P, DC, HALF, DM])
        inwT = sb("inwT", [DM, DC, E])
        xpw = sb("xpw", [DT0 + DR, E])
        xpwT = sb("xpwT", [P, HALF, DT0 + DR])
        dtw = sb("dtw", [P, HALF, DT0 + DR])
        dtwT = sb("dtwT", [DT0 + DR, E])
        cw = sb("cw", [P, HALF, DC])
        cb = sb("cb", [P, HALF])
        dtb = sb("dtb", [P, HALF])
        dskip = sb("dskip", [P, HALF])
        alog = sb("alog", [P, HALF, DS])
        aneg = sb("aneg", [P, HALF, DS])
        gates = sb("gates", [P, 2])
        tg = sb("tg", [P, 2])
        onesf = sb("onesf", [P, P])
        eps_c = sb("eps_c", [P, 1])
        one_c = sb("one_c", [P, 1])
        magic_c = sb("magic_c", [P, 1])
        zero_c = sb("zero_c", [P, 1])
        st1 = sb("st1", [P, B * LC, 6])
        mv1 = sb("mv1", [P, B * LC, 2])
        ln1 = sb("ln1", [P, B * LC])
        r1 = sb("r1", [P, B * LC])
        nt1 = sb("nt1", [P, B * LC])
        ve1 = sb("ve1", [P, B * LC])
        zn = sb("zn", [P, HALF, L])
        sz = sb("sz", [P, HALF, L])
        szT = sb("szT", [P, LC, E])
        conv = sb("conv", [P, HALF, L])
        u = sb("u", [P, 2, HALF, L])
        bc3 = sb("bc3", [3 * 2 * DS, B, L], BF16)
        res1 = sb("res1", [3 * 2 * DS, L])
        mid = sb("mid", [3 * 2 * DS, L], BF16)
        dtlo = sb("dtlo", [DT0 + DR, L])
        spa = sb("spa", [P, HALF, L])
        spe = sb("spe", [P, HALF, L])
        spl = sb("spl", [P, HALF, L])
        spr = sb("spr", [P, HALF, L])
        spm = spa
        delta = sb("delta", [P, 2, HALF, L])
        du = sb("du", [P, 2, HALF, L])
        skip = sb("skip", [P, 2, HALF, L])
        Bs = sb("Bs", [P, RING, NB, L])
        decay = sb("decay", [P, RING, HALF, NB, L])
        drive = sb("drive", [P, RING, HALF, NB, L])
        state = sb("state", [P, STATES, HALF, NB, L])
        prod = sb("prod", [P, RING, HALF, NB, L])
        x2 = sb("x2", [P, 2, LC, E])
        st2 = sb("st2", [P, LC, 6])
        mv2 = sb("mv2", [P, LC, 2])
        ve2 = sb("ve2", [P, LC])
        ln2 = sb("ln2", [P, LC])
        r2 = sb("r2", [P, LC])
        nt2 = sb("nt2", [P, LC])
        xn = sb("xn", [P, LC, E])
        yg = xn
        amax = sb("amax", [P, LC])
        ainv = sb("ainv", [P, LC])
        gs = sb("gs", [P, LC])
        us = sb("us", [P, LC])
        q = sb("q", [P, LC, E], BF16)
        qT = sb("qT", [P, HALF, L], BF16)
        wnat = sb("wnat", [P, 3, 2 * I])
        wq = sb("wq", [P, 3, 2 * I], BF16)
        wT = sb("wT", [P, 3, 2 * I], BF16)
        hT = sb("hT", [P, LC, NI, P])
        wabs = hT[:].rearrange("p t a c -> p (t a c)")
        wsum = sb("wsum", [P, 3])
        wmean = sb("wmean", [P, 3])
        winv = sb("winv", [P, 3])
        wdn = sb("wdn", [P, 1])
        inter = wnat[:, 0].rearrange("p (t n) -> p t n", t=LC)
        had2 = wnat[:, 2, 0:4 * P].rearrange("p (j i c) -> p j i c", j=2, i=2)
        fold = wnat[:, 1].rearrange("p (t n) -> p t n", t=LC)
        sg = wq[:, 0:2].rearrange("p m n -> p (m n)").bitcast(F32).rearrange("p (t n) -> p t n", t=LC)
        am2 = sb("am2", [P, LC])
        sc2 = sb("sc2", [P, LC])
        dq2 = sb("dq2", [P, LC])
        tq = ctxs[:].rearrange("p b c d -> p (b c d)")
        q2 = wq[:, 2].rearrange("p (t n) -> p t n", t=LC)
        q2T = sb("q2T", [P, LC, NI, P], BF16)
        ot = sb("ot", [P, LC, E])

        PB, PC, PY = (stack.enter_context(nc.psum_tensor(n, [P, w], F32)) for n, w in
                      (("PB", 512), ("PC", 512), ("PY", 512)))
        pairs = [stack.enter_context(nc.psum_tensor(f"pair{i}", [P, 2 * 512], F32)) for i in range(2)]
        GP, UP = pairs
        X = stack.enter_context(nc.psum_tensor("X", [P, 512], F32))[:]
        bank4, bank5 = GP[:, 0:512], GP[:, 512:1024]
        bank6, bank7 = UP[:, 0:512], UP[:, 512:1024]

        wgT = wT[:, 0].rearrange("p (h i) -> p h i", h=HALF)
        wuT = wT[:, 1].rearrange("p (h i) -> p h i", h=HALF)
        wdT = wT[:, 2].rearrange("p (a o) -> p a o", a=NI)

        ld_consts, ld_ctx0, ld_inw, ld_small, ld_ctx, ld_x, ld_had, ld_gate = (
            sem(n) for n in ("ld_consts", "ld_ctx0", "ld_inw", "ld_small", "ld_ctx", "ld_x", "ld_had", "ld_gate"))
        ld_conv, ld_w = sem("ld_conv"), [sem(f"ld_w{i}") for i in range(3)]
        zeroed, consts, decay_zeroed = sem("zeroed"), sem("consts"), sem("decay_zeroed")
        pe_setup, act_setup, dve_setup = sem("pe_setup"), sem("act_setup"), sem("dve_setup")
        act_gate, dve_aneg, dve_consts = sem("act_gate"), sem("dve_aneg"), sem("dve_consts")
        dve_stat1, act_r1, dve_r1 = sem("dve_stat1"), sem("act_r1"), sem("dve_r1")
        wabs_done, pe_wsum, dve_winv, pool_wt, dve_wq, pe_wT, dve_wT = (
            sem(n) for n in ("wabs_done", "pe_wsum", "dve_winv", "pool_wt", "dve_wq", "pe_wT", "dve_wT"))
        pe_B, act_B, act_decay, pool_drive, dve_scan, pe_C, dve_prod, pe_acc = (
            sem(n) for n in ("pe_B", "act_B", "act_decay", "pool_drive", "dve_scan", "pe_C", "dve_prod", "pe_acc"))
        pe_xin, dve_inwk, act_conv, act_u, pe_xdbl, dve_split, act_dtlo, pe_draw = (
            sem(n) for n in ("pe_xin", "dve_inwk", "act_conv", "act_u", "pe_xdbl", "dve_split", "act_dtlo", "pe_draw"))
        act_spread, act_sp, delta_ready, du_ready, dve_zn, act_sz, pe_szT, act_szT, pe_y, dve_x2 = (
            sem(n) for n in ("act_spread", "act_sp", "delta_ready", "du_ready", "dve_zn", "act_sz", "pe_szT", "act_szT",
                             "pe_y", "dve_x2"))
        dve_stat2, act_r2, dve_q, pe_qT, dve_qT, pe_gate, pe_up, act_sg, dve_mul = (
            sem(n) for n in ("dve_stat2", "act_r2", "dve_q", "pe_qT", "dve_qT", "pe_gate", "pe_up", "act_sg", "dve_mul"))
        pool_fold, pe_tp, act_tp, pe_h, dve_sc, act_tq, dve_q2, pe_q2T, dve_q2T, pe_dn, dve_out = (
            sem(n) for n in ("pool_fold", "pe_tp", "act_tp", "pe_h", "dve_sc", "act_tq", "dve_q2", "pe_q2T", "dve_q2T",
                             "pe_dn", "dve_out"))
        stored = [sem(f"stored_{t}") for t in range(LC)]
        pool_front_link = Chain(sem("pool_front_link"), 4)
        dve_front_link = Chain(sem("dve_front_link"), 4)
        had_built = sem("had_built")
        dve_once = sem("dve_once")
        act_r2_link = Chain(sem("act_r2_link"), 1)
        act_sp_link = Chain(sem("act_sp_link"), 1)
        pool_stage = sem("pool_stage")
        dve_split_link = Chain(sem("dve_split_link"), 3)
        dve_gs, dve_dq = sem("dve_gs"), sem("dve_dq")
        dve_ln_link = Chain(sem("dve_ln_link"), 11)
        dve_sc_link = Chain(sem("dve_sc_link"), 2)

        block = stack.enter_context(nc.Block())

        def front_bank(n):
            return bank4 if n < 2 else X

        def softplus_tail(n, eng, ops, link, part):
            if part == 0:
                eng.wait_ge(act_sp, n + 1)
                link(ops.tensor_scalar(spm[:], spe[:], 1.0, 1.0, ALU.mult, ALU.add))
                link(ops.tensor_scalar(spm[:], spm[:], 1.0, -1.0, ALU.mult, ALU.add))
                link(ops.tensor_tensor(spm[:], spm[:], spe[:], ALU.subtract))
            if part == 1:
                if n >= 2:
                    eng.wait_ge(act_decay, STEPS * (n - 1))
                link(ops.tensor_tensor(spl[:], spl[:], spm[:], ALU.subtract))
                ops.tensor_tensor(delta[:, n % 2], spl[:], spr[:], ALU.add).then_inc(delta_ready, 1)
            if part == 2:
                if n >= 2:
                    eng.wait_ge(pe_y, n - 1)
                    eng.wait_ge(pool_drive, STEPS * (n - 1))
                for h in range(HALF):
                    ops.tensor_scalar(skip[:, n % 2, h], u[:, n % 2, h], dskip[:, h:h + 1], 1.0, ALU.mult, ALU.mult)
                eng.wait_ge(delta_ready, n + 1)
                ops.tensor_tensor(du[:, n % 2], delta[:, n % 2], u[:, n % 2], ALU.mult).then_inc(du_ready, 1)
                link.end()

        @block.sync
        def _(sp):
            rows = x_rows(x)
            cr = x_rows(ctx_1024)
            sp.dma_start(ctxs[:, 0], cr[0]).then_inc(ld_ctx0, 16)
            sp.dma_start(inw[:], in_proj_w.rearrange("(h p) d -> p h d", p=P)).then_inc(ld_inw, 16)
            for i in range(3):
                sp.dma_start(xpw[2 * DS * i:2 * DS * (i + 1), :], x_proj_w[DR:DR + 2 * DS, :]).then_inc(ld_small, 16)
            sp.dma_start(xpw[DT0:DT0 + DR, :], x_proj_w[0:DR, :]).then_inc(ld_small, 16)
            sp.wait_ge(zeroed, 1)
            sp.dma_start(dtw[:, :, DT0:DT0 + DR], dt_proj_w.rearrange("(h p) r -> p h r", p=P)).then_inc(ld_small, 16)
            sp.dma_start(wnat[:, 0].rearrange("p (a h) -> p a h", a=NI),
                         w_gate.rearrange("(a p) h -> p a h", p=P)).then_inc(ld_w[0], 16)
            sp.dma_start(wnat[:, 1].rearrange("p (a h) -> p a h", a=NI),
                         w_up.rearrange("(a p) h -> p a h", p=P)).then_inc(ld_w[1], 16)
            for b in range(B):
                sp.dma_start(xs[:, b], rows[b]).then_inc(ld_x, 16)
            sp.dma_start(wnat[:, 2].rearrange("p (o i) -> p o i", o=HALF),
                         w_down.rearrange("(o p) i -> p o i", p=P)).then_inc(ld_w[2], 16)
            for b in range(1, B):
                sp.dma_start(ctxs[:, b], cr[b]).then_inc(ld_ctx, 16)
            sp.dma_start(had[:], hadamard).then_inc(ld_had, 16)
            for b in range(B):
                for t in range(LC):
                    sp.wait_ge(dve_out, LC * b + t + 1)
                    sp.dma_start(x_rows(out)[b][:, t], ot[:, t]).then_inc(stored[t], 16)
            for t in range(LC):
                sp.wait_ge(stored[t], 16 * B)

        @block.tensor
        def _(pe):
            def setup():
                pe.wait_ge(ld_consts, 16)
                pe.wait_ge(ld_ctx0, 16)
                for c in range(LC):
                    last = nc.tensor.transpose(bank4[:, P * c:P * (c + 1)], ctxs[:, 0, c], id32[:])
                last.then_inc(pe_setup, 1)
                pe.wait_ge(dve_inwk, 1)
                for k in range(DC):
                    for h in range(HALF):
                        last = nc.tensor.transpose(UP[:, E * k + P * h:E * k + P * (h + 1)], inwk[:, k, h], id32[:])
                last.then_inc(pe_setup, 1)
                pe.wait_ge(ld_small, 16 * 5)
                for h in range(HALF):
                    last = nc.tensor.transpose(bank5[:, P * h:P * h + DT0 + DR], xpw[:, P * h:P * (h + 1)],
                                               id32[0:DT0 + DR, 0:DT0 + DR])
                last.then_inc(pe_setup, 1)
                for h in range(HALF):
                    last = nc.tensor.transpose(PB[0:DT0 + DR, P * h:P * (h + 1)], dtw[:, h], id32[:])
                last.then_inc(pe_setup, 1)

            def setup_late():
                pe.wait_ge(ld_ctx, 16 * (B - 1))
                for b in range(1, B):
                    for c in range(LC):
                        at = (b - 1) * L + P * c
                        last = nc.tensor.transpose((PC if at < 512 else PY)[:, at % 512:at % 512 + P], ctxs[:, b, c], id32[:])
                last.then_inc(pe_setup, 1)

            def B_rows(m):
                b, j = divmod(m, STEPS)
                pe.wait_ge(dve_split, b + 1)
                if m >= 1:
                    pe.wait_ge(act_B, m)
                else:
                    pe.wait_ge(act_setup, 4)
                for n in range(NB):
                    last = nc.tensor.matmul(PB[:, L * n:L * (n + 1)], row_pick(NB * j + n), bc3[:, b, :],
                                            start=True, stop=True)
                last.then_inc(pe_B, 1)

            def C_rows(m):
                b, j = divmod(m, STEPS)
                pe.wait_ge(dve_split, b + 1)
                if m >= 1:
                    pe.wait_ge(dve_prod, m)
                else:
                    pe.wait_ge(act_setup, 5)
                for n in range(NB):
                    last = nc.tensor.matmul(PC[:, L * n:L * (n + 1)], row_pick(DS + NB * j + n), bc3[:, b, :],
                                            start=True, stop=True)
                last.then_inc(pe_C, 1)

            def row_pick(r):
                return sel[:, r:r + 1].to_broadcast([3 * 2 * DS, P])

            def accumulate(g):
                b, j = divmod(g, STEPS)
                pe.wait_ge(dve_prod, g + 1)
                if j == 0 and b >= 1:
                    pe.wait_ge(dve_x2, b)
                for h in range(HALF):
                    for n in range(NB):
                        for c in range(LC):
                            last = nc.tensor.matmul(PY[:, E * c + P * h:E * c + P * (h + 1)],
                                                    prod[:, g % RING, h, n, P * c:P * (c + 1)], id32[:],
                                                    is_transpose=True, start=(j == 0 and h == n == c == 0), stop=False,
                                                    skip_group_check=True)
                last.then_inc(pe_acc, 1)
                if j == STEPS - 1:
                    pe.wait_ge(du_ready, b + 1)
                    for h in range(HALF):
                        for c in range(LC):
                            last = nc.tensor.matmul(PY[:, E * c + P * h:E * c + P * (h + 1)],
                                                    skip[:, b % 2, h, P * c:P * (c + 1)], id32[:],
                                                    is_transpose=True, start=False, stop=(h == HALF - 1 and c == LC - 1),
                                                    skip_group_check=True)
                    last.then_inc(pe_y, 1)

            def in_proj(n):
                if n == 0:
                    pe.wait_ge(act_setup, 2)
                elif n == 1:
                    pe.wait_ge(act_setup, 5)
                    pe.wait_ge(act_spread, n)
                elif n == 2:
                    pass
                else:
                    pe.wait_ge(dve_qT, n - 2)
                for h in range(HALF):
                    for d in range(DC):
                        last = nc.tensor.matmul(front_bank(n)[:, L * h + d:L * (h + 1)],
                                                inwT[:, DC - 1 - d, P * h:P * (h + 1)], ctxT[:, n, 0:L - d],
                                                start=(d == 0), stop=(d == DC - 1))
                last.then_inc(pe_xin, 1)

            def x_dbl(n):
                pe.wait_ge(act_u, n + 1)
                if n == 0:
                    pe.wait_ge(act_setup, 3)
                if n >= 2:
                    pe.wait_ge(act_conv, n - 1)
                if n >= 4:
                    pe.wait_ge(dve_out, LC * (n - 3))
                for h in range(HALF):
                    last = nc.tensor.matmul(front_bank(n)[0:DT0 + DR, 0:L], xpwT[:, h, :], u[:, n % 2, h, :],
                                            start=(h == 0), stop=(h == HALF - 1))
                last.then_inc(pe_xdbl, 1)

            def dt_proj(n):
                pe.wait_ge(act_dtlo, n + 1)
                pe.wait_ge(dve_split, n + 1)
                if n == 0:
                    pe.wait_ge(act_setup, 4)
                for h in range(HALF):
                    last = nc.tensor.matmul(front_bank(n)[:, L * h:L * (h + 1)], dtwT[DT0:DT0 + DR, P * h:P * (h + 1)],
                                            dtlo[DT0:DT0 + DR, :], start=True, stop=True)
                last.then_inc(pe_draw, 1)

            def gate_T(k):
                pe.wait_ge(act_sz, k + 1)
                if k >= 1 and k + 1 < B:
                    pe.wait_ge(act_spread, k + 2)
                if k + 1 == B:
                    pe.wait_ge(dve_out, LC * (k - 2))
                for h in range(HALF):
                    for c in range(LC):
                        last = nc.tensor.transpose((bank5 if k == 0 else X)[:, E * c + P * h:E * c + P * (h + 1)],
                                                   sz[:, h, P * c:P * (c + 1)], id32[:])
                last.then_inc(pe_szT, 1)

            def tokens_T(f):
                pe.wait_ge(dve_q, f + 1)
                if f + 1 < B:
                    pe.wait_ge(act_szT, f + 2)
                else:
                    pe.wait_ge(dve_out, LC * (f - 1))
                for c in range(LC):
                    for h in range(HALF):
                        last = nc.tensor.transpose(X.bitcast(BF16)[:, L * h + P * c:L * h + P * (c + 1)],
                                                   q[:, c, P * h:P * (h + 1)], id16[:])
                last.then_inc(pe_qT, 1)

            def gate_up(f, t):
                pe.wait_ge(dve_qT, f + 1)
                if t == 1:
                    pe.wait_ge(act_sg, LC * f + 1)
                elif f >= 1:
                    pe.wait_ge(dve_out, LC * (f - 1) + 1)
                else:
                    pe.wait_ge(act_spread, 2)
                    pe.wait_ge(act_szT, 1)
                for bks, w, done in ((GP, wgT, pe_gate), (UP, wuT, pe_up)):
                    if done is pe_up:
                        if t == 1:
                            pe.wait_ge(dve_mul, LC * f + 1)
                        elif f >= 1:
                            pe.wait_ge(act_tq, LC * f)
                        else:
                            pe.wait_ge(dve_wT, 6)
                    elif f == t == 0:
                        pe.wait_ge(dve_wT, 6)
                    for i in range(2):
                        for h in range(HALF):
                            last = nc.tensor.matmul(bks[:, 512 * i:512 * (i + 1)], qT[:, h, P * t:P * (t + 1)],
                                                    w[:, h, 512 * i:512 * (i + 1)],
                                                    start=(h == 0), stop=(h == HALF - 1))
                    last.then_inc(done, 1)

            def inter_T(f, t):
                pe.wait_ge(pool_fold, LC * f + t + 1)
                if t == 0:
                    pe.wait_ge(act_sg, LC * f + 2)
                else:
                    pe.wait_ge(act_tp, LC * f + 1)
                for a in range(NI):
                    last = nc.tensor.transpose(GP[:, P * a:P * (a + 1)], inter[:, t, P * a:P * (a + 1)], id32[:])
                last.then_inc(pe_tp, 1)

            def hadamard_mm(f, t):
                pe.wait_ge(act_tp, LC * f + t + 1)
                if f == t == 0:
                    pe.wait_ge(had_built, 1)
                if t == 0:
                    pe.wait_ge(dve_mul, LC * f + 2)
                else:
                    pe.wait_ge(act_tq, LC * f + 1)
                for a in range(NI):
                    last = nc.tensor.matmul(UP[:, E * (a // 2):E * (a // 2 + 1)], hT[:, t, a, :],
                                            had2[:, a % 2].rearrange("p i c -> p (i c)"),
                                            start=(a % 2 == 0), stop=(a % 2 == 1))
                last.then_inc(pe_h, 1)

            def q2_T(f, t, n):
                pe.wait_ge(dve_q2, LC * f + t + 1)
                if t == 0:
                    pe.wait_ge(act_tp, LC * f + 2)
                else:
                    if n < B:
                        pe.wait_ge(act_conv, n - 1)
                    pe.wait_ge(dve_qT, min(f + 2, B))
                for a in range(NI):
                    last = nc.tensor.transpose((bank4 if t == 0 else X).bitcast(BF16)[:, P * a:P * (a + 1)],
                                               q2[:, t, P * a:P * (a + 1)], id16[:])
                last.then_inc(pe_q2T, 1)

            def down(f, t):
                pe.wait_ge(dve_q2T, LC * f + t + 1)
                for a in range(NI):
                    last = nc.tensor.matmul((bank5 if t == 0 else X)[:, 0:E], q2T[:, t, a, :], wdT[:, a, :],
                                            start=(a == 0), stop=(a == NI - 1))
                last.then_inc(pe_dn, 1)

            def weight_sum():
                pe.wait_ge(wabs_done, 3)
                pe.wait_ge(act_setup, 2)
                nc.tensor.matmul(bank7[:, 0:3], onesf[:], wsum[:], start=True, stop=True).then_inc(pe_wsum, 1)

            def weight_T(i):
                m, part = divmod(i, 2)
                pe.wait_ge(dve_wq, m + 1)
                if i == 0:
                    pe.wait_ge(dve_winv, 1)
                if i >= 2:
                    pe.wait_ge(dve_wT, i - 1)
                bk = (bank7 if i % 2 == 0 else bank6).bitcast(BF16)
                for k in range(8):
                    if m < 2:
                        blk = wq[:, m].rearrange("p (a h c) -> p h a c", a=NI, h=HALF)[:, part, k, :]
                    else:
                        a, oh = 4 * part + k // 2, k % 2
                        blk = wq[:, m].rearrange("p (o a c) -> p o a c", o=HALF, a=NI)[:, oh, a, :]
                    last = nc.tensor.transpose(bk[:, P * k:P * (k + 1)], blk, id16[:])
                last.then_inc(pe_wT, 1)

            setup()
            in_proj(0)
            setup_late()
            pe.wait_ge(dve_consts, 1)
            x_dbl(0)
            dt_proj(0)
            B_rows(0)
            C_rows(0)
            for m in range(1, AHEAD):
                B_rows(m)
            for k in range(B + 2):
                p, f, n = k - 2, k - 1, k + 2
                old, new, front = p >= 0, 0 <= f < B, n < B
                for s in range(STEPS):
                    g = STEPS * k + s
                    if g + AHEAD < B * STEPS:
                        B_rows(g + AHEAD)
                    if s == 0:
                        if old:
                            hadamard_mm(p, 0)
                        if k == 0:
                            in_proj(1)
                    if s == 1:
                        if 1 <= k < B:
                            gate_T(k)
                        if old:
                            inter_T(p, 1)
                        if k == 0:
                            weight_sum()
                    if s == 2:
                        if new:
                            tokens_T(f)
                        if old:
                            hadamard_mm(p, 1)
                            q2_T(p, 0, n)
                        if k == 0:
                            x_dbl(1)
                    if s == 3:
                        if old:
                            down(p, 0)
                        if k == 0:
                            dt_proj(1)
                        if front:
                            in_proj(n)
                    if s == 4:
                        if old:
                            q2_T(p, 1, n)
                        if new:
                            gate_up(f, 0)
                        if k == 0:
                            gate_T(0)
                    if s == 5:
                        if new:
                            gate_up(f, 1)
                        if old:
                            down(p, 1)
                    if s == 6 and front:
                        x_dbl(n)
                    if s == 7:
                        if front:
                            dt_proj(n)
                        if new:
                            inter_T(f, 0)
                    if k == 0 and s >= 4:
                        for i in ((0, 1), (2,), (3, 4), (5,))[s - 4]:
                            weight_T(i)
                    if k < B:
                        if g + 1 < B * STEPS:
                            C_rows(g + 1)
                        accumulate(g)

        @block.scalar
        def _(act):
            def setup_loads():
                act.dma_start(id32[:], ident).then_inc(ld_consts, 16)
                act.dma_start(cw[:], conv_w.rearrange("(h p) k -> p h k", p=P)).then_inc(ld_conv, 16)
                for dst, src in ((cb, conv_b), (dtb, dt_proj_b), (dskip, D)):
                    with nc.allow_non_contiguous_dma(reason="one value per partition"):
                        act.dma_start(dst[:], src.rearrange("(h p) -> p h", p=P)).then_inc(ld_conv, 16)
                act.dma_start(alog[:], A_log.rearrange("(h p) n -> p h n", p=P)).then_inc(ld_gate, 16)
                act.dma_start(gates[:, 0:1], g_xattn.partition_broadcast(P)).then_inc(ld_gate, 16)
                act.dma_start(gates[:, 1:2], g_ffn.partition_broadcast(P)).then_inc(ld_gate, 16)

            def copy_B(m):
                act.wait_ge(pe_B, m + 1)
                if m >= RING:
                    act.wait_ge(pool_drive, m - RING + 1)
                nc.scalar.copy(Bs[:, m % RING], PB[:].rearrange("p (n l) -> p n l", n=NB)).then_inc(act_B, 1)

            def decays(m):
                b, j = divmod(m, STEPS)
                act.wait_ge(delta_ready, b + 1)
                if m >= RING:
                    act.wait_ge(dve_scan, m - RING + 1)
                for h in range(HALF):
                    for n in range(NB):
                        last = nc.scalar.activation(decay[:, m % RING, h, n, 1:L], delta[:, b % 2, h, 1:L], ACT.Exp,
                                                    bias=zero_c[:], scale=aneg[:, h, NB * j + n:NB * j + n + 1])
                last.then_inc(act_decay, 1)

            def conv_out(n):
                act.wait_ge(pe_xin, n + 1)
                if n >= 3:
                    act.wait_ge(act_u, n)
                for h in range(HALF):
                    last = nc.scalar.activation(conv[:, h, :], X[:, L * h:L * (h + 1)], ACT.Identity, bias=cb[:, h:h + 1])
                last.then_inc(act_conv, 1)

            def silu_u(n):
                if n < 2:
                    act.wait_ge(pe_xin, n + 1)
                    for h in range(HALF):
                        last = nc.scalar.activation(u[:, n, h], bank4[:, L * h:L * (h + 1)], ACT.Silu, bias=cb[:, h:h + 1])
                    last.then_inc(act_u, 1)
                else:
                    act.wait_ge(act_conv, n - 1)
                    act.wait_ge(pe_xdbl, n - 1)
                    act.wait_ge(du_ready, n - 1)
                    nc.scalar.activation(u[:, n % 2], conv[:], ACT.Silu, bias=zero_c[:]).then_inc(act_u, 1)

            def silu_z(n):
                act.wait_ge(dve_zn, n + 1)
                if n >= 1:
                    act.wait_ge(pe_szT, n)
                nc.scalar.activation(sz[:], zn[:], ACT.Silu, bias=zero_c[:]).then_inc(act_sz, 1)

            def dt_rows(n):
                act.wait_ge(pe_xdbl, n + 1)
                nc.scalar.copy(dtlo[DT0:DT0 + DR, :], front_bank(n)[DT0:DT0 + DR, 0:L]).then_inc(act_dtlo, 1)

            def softplus(n):
                link = act_sp_link.begin(act, n)
                act.wait_ge(pe_draw, n + 1)
                if n >= 1:
                    act.wait_ge(delta_ready, n)
                for h in range(HALF):
                    v = front_bank(n)[:, L * h:L * (h + 1)]
                    nc.scalar.activation(spr[:, h], v, ACT.Relu, bias=dtb[:, h:h + 1])
                    last = nc.scalar.activation(spa[:, h], v, ACT.Abs, bias=dtb[:, h:h + 1])
                last.then_inc(act_spread, 1)
                act.wait_ge(act_spread, n + 1)
                link(nc.scalar.activation(spe[:], spa[:], ACT.Exp, bias=zero_c[:], scale=-1.0))
                nc.scalar.activation(spl[:], spe[:], ACT.Ln, bias=one_c[:]).then_inc(act_sp, 1)
                link.end()

            def gate_out(k):
                act.wait_ge(pe_szT, k + 1)
                if k >= 1:
                    act.wait_ge(dve_x2, k)
                nc.scalar.activation(szT[:], (bank5 if k == 0 else X).rearrange("p (c e) -> p c e", c=LC), ACT.Copy,
                                     scale=tg[:, 0:1]).then_inc(act_szT, 1)

            def rstd2(f):
                link = act_r2_link.begin(act, f)
                act.wait_ge(dve_stat2, f + 1)
                link(nc.scalar.activation(ln2[:], mv2[:, :, 1], ACT.Ln, bias=eps_c[:]))
                nc.scalar.activation(r2[:], ln2[:], ACT.Exp, bias=zero_c[:], scale=-0.5).then_inc(act_r2, 1)
                link.end()

            def silu_gate(f, t):
                act.wait_ge(pe_gate, LC * f + t + 1)
                act.wait_ge(dve_gs, f + 1)
                nc.scalar.activation(sg[:, t], GP[:], ACT.Silu, bias=zero_c[:], scale=gs[:, t:t + 1]).then_inc(act_sg, 1)

            def inter_out(f, t):
                act.wait_ge(pe_tp, LC * f + t + 1)
                nc.scalar.copy(hT[:, t].rearrange("p a c -> p (a c)"), GP[:]).then_inc(act_tp, 1)

            def quant_down(f, t):
                act.wait_ge(dve_sc, LC * f + t + 1)
                if LC * f + t >= 1:
                    act.wait_ge(dve_q2, LC * f + t)
                nc.scalar.activation(tq, UP[:], ACT.Identity, bias=magic_c[:], scale=sc2[:, t:t + 1]
                                     ).then_inc(act_tq, 1)

            def weight_abs(m):
                act.wait_ge(ld_w[m], 16)
                if m == 2:
                    act.wait_ge(wabs_done, 1)
                nc.scalar.activation(wabs, wnat[:, m], ACT.Abs, bias=zero_c[:],
                                     accum_out=wsum[:, m:m + 1]).then_inc(wabs_done, 1)

            def for_silu():
                nc.scalar.preload_act_table_set("silu_and_others")

            def for_exp():
                nc.scalar.preload_act_table_set("natural_log_exp_and_others")

            setup_loads()
            for_silu()
            act.wait_ge(consts, 1)
            act.wait_ge(pe_setup, 1)
            nc.scalar.copy(ctxT[:, 0], bank4[:, 0:L]).then_inc(act_setup, 1)
            act.wait_ge(pe_setup, 2)
            nc.scalar.copy(inwT[:].rearrange("p k e -> p (k e)"), UP[:]).then_inc(act_setup, 1)
            act.wait_ge(pe_setup, 3)
            nc.scalar.copy(xpwT[:], bank5[:, 0:HALF * P].rearrange("p (h k) -> p h k", h=HALF)[:, :, 0:DT0 + DR]
                           ).then_inc(act_setup, 1)
            act.wait_ge(pe_setup, 4)
            nc.scalar.copy(dtwT[DT0:DT0 + DR, :], PB[DT0:DT0 + DR, 0:E]).then_inc(act_setup, 1)
            act.wait_ge(ld_conv, 16 * 4)
            silu_u(0)
            act.wait_ge(ld_gate, 16 * 3)
            nc.scalar.activation(tg[:], gates[:], ACT.Tanh, bias=zero_c[:]).then_inc(act_gate, 1)
            for_exp()
            dt_rows(0)
            nc.scalar.activation(aneg[:], alog[:], ACT.Exp, bias=zero_c[:]).then_inc(act_gate, 1)
            softplus(0)
            act.wait_ge(pe_setup, 5)
            nc.scalar.copy(ctxT[:, 1:3], PC[:].rearrange("p (b l) -> p b l", b=2))
            nc.scalar.copy(ctxT[:, 3], PY[:, 0:L]).then_inc(act_setup, 1)
            act.wait_ge(dve_aneg, 1)
            act.wait_ge(decay_zeroed, 1)
            for m in range(AHEAD):
                copy_B(m)
                decays(m)
            for k in range(B + 2):
                p, f, n = k - 2, k - 1, k + 2
                old, new, front = p >= 0, 0 <= f < B, n < B
                for s in range(STEPS):
                    g = STEPS * k + s
                    if g + AHEAD < B * STEPS:
                        copy_B(g + AHEAD)
                        decays(g + AHEAD)
                    if s == 0:
                        if new:
                            rstd2(f)
                        if k == 0:
                            weight_abs(0)
                            act.wait_ge(dve_stat1, 1)
                            nc.scalar.activation(ln1[:], mv1[:, :, 1], ACT.Ln, bias=eps_c[:]).then_inc(act_r1, 1)
                            act.wait_ge(act_r1, 1)
                            nc.scalar.activation(r1[:], ln1[:], ACT.Exp, bias=zero_c[:], scale=-0.5).then_inc(act_r1, 1)
                    if s == 1:
                        if 1 <= k < B:
                            gate_out(k)
                        if old:
                            inter_out(p, 1)
                            quant_down(p, 0)
                        if k == 0:
                            for_silu()
                            silu_u(1)
                            silu_z(0)
                            for_exp()
                    if s == 2 and k == 0:
                        dt_rows(1)
                    if s == 3:
                        if k == 0:
                            softplus(1)
                        if front:
                            conv_out(n)
                        if old:
                            quant_down(p, 1)
                    if s == 5:
                        if k == 0:
                            gate_out(0)
                        if new or front:
                            for_silu()
                        if new:
                            silu_gate(f, 0)
                        if front:
                            silu_u(n)
                        if k + 1 < B:
                            silu_z(k + 1)
                        if new:
                            silu_gate(f, 1)
                        if k < B:
                            for_exp()
                    if s == 6 and front:
                        dt_rows(n)
                    if s == 7:
                        if new:
                            inter_out(f, 0)
                        if front:
                            softplus(n)

        @block.gpsimd
        def _(pool):
            def drives(m):
                b, j = divmod(m, STEPS)
                pool.wait_ge(act_B, m + 1)
                pool.wait_ge(du_ready, b + 1)
                if m >= RING:
                    pool.wait_ge(dve_scan, m - RING + 1)
                for h in range(HALF):
                    last = nc.gpsimd.tensor_tensor(
                        drive[:, m % RING, h], du[:, b % 2, h, :].unsqueeze(1).to_broadcast([P, NB, L]),
                        Bs[:, m % RING], ALU.mult)
                last.then_inc(pool_drive, 1)

            def fold_tile(f, t, stage):
                if stage == 0:
                    pool.wait_ge(dve_mul, LC * f + t + 1)
                    src, dst, done, gap = inter, fold, pool_stage, 4
                else:
                    pool.wait_ge(pool_stage, LC * f + t + 1)
                    src, dst, done, gap = fold, inter, pool_fold, 2
                src, dst = (v[:, t].rearrange("p (g s w) -> p g s w", s=2, w=gap * P) for v in (src, dst))
                nc.gpsimd.tensor_tensor(dst[:, :, 0, :], src[:, :, 0, :], src[:, :, 1, :], ALU.add)
                nc.gpsimd.tensor_tensor(dst[:, :, 1, :], src[:, :, 0, :], src[:, :, 1, :], ALU.subtract).then_inc(done, 1)

            def weight_scale(m):
                pool.wait_ge(dve_winv, 1)
                pool.wait_ge(ld_w[m], 16)
                nc.gpsimd.tensor_scalar(wnat[:, m], wnat[:, m], winv[:, m:m + 1], MAGIC, ALU.mult, ALU.add
                                        ).then_inc(pool_wt, 1)

            def build_hadamard():
                pool.wait_ge(ld_had, 16)
                pool.wait_ge(dve_wq, 3)
                v = had2.rearrange("p j i c -> p (j i) c")
                nc.gpsimd.tensor_copy(v[:, 0:3], had[:].unsqueeze(1).to_broadcast([P, 3, P]))
                nc.gpsimd.tensor_scalar(v[:, 3], had[:], -1.0, 1.0, ALU.mult, ALU.mult).then_inc(had_built, 1)

            nc.gpsimd.memset(dtw[:], 0.0).then_inc(zeroed, 1)
            nc.gpsimd.memset(zero_c[:], 0.0)
            nc.gpsimd.memset(one_c[:], 1.0)
            nc.gpsimd.memset(eps_c[:], LN_EPS)
            nc.gpsimd.memset(onesf[:], 1.0)
            nc.gpsimd.memset(magic_c[:], MAGIC).then_inc(consts, 1)
            for r in range(RING):
                last = nc.gpsimd.memset(decay[:, r, :, :, 0:1], 0.0)
            last.then_inc(decay_zeroed, 1)
            for m in range(AHEAD):
                drives(m)
            for k in range(B + 2):
                p, f, n = k - 2, k - 1, k + 1
                for s in range(STEPS):
                    g = STEPS * k + s
                    if g + AHEAD < B * STEPS:
                        drives(g + AHEAD)
                    if k == 0:
                        if 2 <= s < 5:
                            weight_scale(s - 2)
                        if s == 6:
                            build_hadamard()
                    if 2 <= n < B and 2 <= s < 5:
                        if s == 2:
                            pool_front_link.begin(pool, n - 2)
                        softplus_tail(n, pool, nc.gpsimd, pool_front_link, s - 2)
                    if 0 <= f < B:
                        if s == 6:
                            fold_tile(f, 0, 0)
                            fold_tile(f, 0, 1)
                        if s == 7:
                            fold_tile(f, 1, 0)
                    if p >= 0 and s == 0:
                        fold_tile(p, 1, 1)

        @block.vector
        def _(dve):
            once = [0]

            def link_once(ins):
                once[0] += 1
                ins.then_inc(dve_once, 1)
                dve.wait_ge(dve_once, once[0])

            def newton(link, r, v, tmp):
                link(nc.vector.scalar_tensor_tensor(out=tmp, in0=r, scalar=-0.5, in1=v, op0=ALU.mult, op1=ALU.mult))
                link(nc.vector.tensor_tensor(tmp, tmp, r, ALU.mult))
                return nc.vector.scalar_tensor_tensor(out=r, in0=tmp, scalar=1.5, in1=r, op0=ALU.add, op1=ALU.mult)

            def scan(g):
                dve.wait_ge(act_decay, g + 1)
                dve.wait_ge(pool_drive, g + 1)
                if g >= STATES:
                    dve.wait_ge(dve_prod, g - STATES + 1)
                nc.vector.tensor_tensor_scan(
                    state[:, g % STATES].rearrange("p h n l -> p (h n l)"), decay[:, g % RING].rearrange("p h n l -> p (h n l)"),
                    drive[:, g % RING].rearrange("p h n l -> p (h n l)"), 0.0, ALU.mult, ALU.add).then_inc(dve_scan, 1)

            def times_C(g):
                dve.wait_ge(dve_scan, g + 1)
                dve.wait_ge(pe_C, g + 1)
                if g >= RING:
                    dve.wait_ge(pe_acc, g - RING + 1)
                nc.vector.tensor_tensor(
                    prod[:, g % RING].rearrange("p h n l -> p h (n l)"),
                    state[:, g % STATES].rearrange("p h n l -> p h (n l)"),
                    PC[:].unsqueeze(1).to_broadcast([P, HALF, NB * L]), ALU.mult).then_inc(dve_prod, 1)

            def norm_z(n):
                dve.wait_ge(dve_r1, 1)
                if n >= 1:
                    dve.wait_ge(act_sz, n)
                for h in range(HALF):
                    i = HALF * n + h
                    last = nc.vector.tensor_scalar(zn[:, h], xs[:, n, h], mv1[:, i, 0:1], r1[:, i:i + 1],
                                                   ALU.subtract, ALU.mult)
                last.then_inc(dve_zn, 1)

            def split(n):
                link = dve_split_link.begin(dve, n)
                k = 2 * DS
                dve.wait_ge(pe_xdbl, n + 1)
                src = front_bank(n)[0:3 * k, 0:L]
                link(nc.vector.tensor_copy(bc3[:, n], src))
                link(nc.vector.tensor_tensor(res1[:], src, bc3[:, n], ALU.subtract))
                nc.vector.tensor_copy(bc3[k:2 * k, n], res1[k:2 * k])
                link(nc.vector.tensor_copy(mid[:], res1[:]))
                nc.vector.tensor_tensor(bc3[2 * k:3 * k, n], res1[2 * k:3 * k], mid[2 * k:3 * k],
                                        ALU.subtract).then_inc(dve_split, 1)
                link.end()

            def residual(f):
                dve.wait_ge(pe_y, f + 1)
                dve.wait_ge(act_szT, f + 1)
                nc.vector.tensor_tensor(yg[:], PY[:].rearrange("p (c e) -> p c e", c=LC), szT[:],
                                        ALU.mult).then_inc(dve_x2, 1)

            def stats2(f, link):
                dve.wait_ge(dve_x2, f + 1)
                link(nc.vector.tensor_tensor(x2[:, f % 2], yg[:], xs[:, f], ALU.add))
                for c in range(LC):
                    ins = nc.vector.bn_stats(st2[:, c], x2[:, f % 2, c])
                link(ins)
                for c in range(LC):
                    ins = nc.vector.bn_aggr(mv2[:, c], st2[:, c])
                ins.then_inc(dve_stat2, 1)

            def quant_tokens(f, link):
                dve.wait_ge(dve_stat2, f + 1)
                link(nc.vector.tensor_scalar(ve2[:], mv2[:, :, 1], LN_EPS, None, ALU.add))
                dve.wait_ge(act_r2, f + 1)
                link(newton(link, r2[:], ve2[:], nt2[:]))
                for c in range(LC):
                    ins = nc.vector.tensor_scalar(xn[:, c], x2[:, f % 2, c], mv2[:, c, 0:1], r2[:, c:c + 1],
                                                  ALU.subtract, ALU.mult)
                link(ins)
                link(nc.vector.tensor_reduce(amax[:], xn[:], AX.X, ALU.max, apply_absolute_value=True))
                link(nc.vector.tensor_scalar(amax[:], amax[:], Q_EPS, 1.0 / QB, ALU.max, ALU.mult))
                link(nc.vector.reciprocal(ainv[:], amax[:]))
                for c in range(LC):
                    ins = nc.vector.tensor_scalar(xn[:, c], xn[:, c], ainv[:, c:c + 1], MAGIC, ALU.mult, ALU.add)
                link(ins)
                nc.vector.tensor_scalar(q[:], xn[:], MAGIC + QB - 1, MAGIC, ALU.min, ALU.subtract).then_inc(dve_q, 1)
                nc.vector.tensor_scalar(gs[:], amax[:], wmean[:, 0:1], None, ALU.mult)
                nc.vector.tensor_scalar(us[:], amax[:], wmean[:, 1:2], None, ALU.mult).then_inc(dve_gs, 1)
                link.end()

            def tokens_out(f):
                dve.wait_ge(pe_qT, f + 1)
                nc.vector.tensor_scalar(qT[:], X.bitcast(BF16)[:, 0:HALF * L].rearrange("p (h l) -> p h l", h=HALF),
                                        -QB, None, ALU.max).then_inc(dve_qT, 1)

            def gate_times_up(f, t):
                dve.wait_ge(act_sg, LC * f + t + 1)
                dve.wait_ge(pe_up, LC * f + t + 1)
                dve.wait_ge(dve_gs, f + 1)
                nc.vector.scalar_tensor_tensor(out=inter[:, t], in0=UP[:], scalar=us[:, t:t + 1], in1=sg[:, t],
                                               op0=ALU.mult, op1=ALU.mult).then_inc(dve_mul, 1)

            def absmax2(f, t):
                link = dve_sc_link.begin(dve, LC * f + t)
                dve.wait_ge(pe_h, LC * f + t + 1)
                a = am2[:, t:t + 1]
                link(nc.vector.tensor_reduce(a, UP[:], AX.X, ALU.max, apply_absolute_value=True))
                link(nc.vector.tensor_scalar(a, a, Q_EPS, 1.0 / QB, ALU.max, ALU.mult))
                nc.vector.reciprocal(sc2[:, t:t + 1], a).then_inc(dve_sc, 1)
                nc.vector.tensor_scalar(dq2[:, t:t + 1], a, wdn[:], None, ALU.mult).then_inc(dve_dq, 1)
                link.end()

            def round_down(f, t):
                dve.wait_ge(act_tq, LC * f + t + 1)
                nc.vector.tensor_scalar(q2[:, t], tq, MAGIC + QB - 1, MAGIC, ALU.min, ALU.subtract).then_inc(dve_q2, 1)

            def q2_out(f, t):
                dve.wait_ge(pe_q2T, LC * f + t + 1)
                nc.vector.tensor_scalar(q2T[:, t], (bank4 if t == 0 else X).bitcast(BF16).rearrange("p (a c) -> p a c", a=NI),
                                        -QB, None, ALU.max).then_inc(dve_q2T, 1)

            def result(f, t):
                dve.wait_ge(pe_dn, LC * f + t + 1)
                dve.wait_ge(dve_dq, LC * f + t + 1)
                if f >= 1:
                    dve.wait_ge(stored[t], 16 * f)
                nc.vector.scalar_tensor_tensor(out=ot[:, t], in0=(bank5 if t == 0 else X)[:, 0:E], scalar=dq2[:, t:t + 1],
                                               in1=x2[:, f % 2, t], op0=ALU.mult, op1=ALU.add).then_inc(dve_out, 1)

            def weight_abs(m):
                dve.wait_ge(ld_w[m], 16)
                nc.vector.tensor_reduce(wsum[:, m:m + 1], wnat[:, m], AX.X, ALU.add,
                                        apply_absolute_value=True).then_inc(wabs_done, 1)

            def weight_means():
                dve.wait_ge(pe_wsum, 1)
                dve.wait_ge(act_gate, 1)
                link_once(nc.vector.tensor_scalar(wmean[:], bank7[:, 0:3], 1.0 / (2 * P * I), Q_EPS, ALU.mult, ALU.max))
                nc.vector.tensor_tensor(wdn[:], wmean[:, 2:3], tg[:, 1:2], ALU.mult)
                nc.vector.reciprocal(winv[:], wmean[:]).then_inc(dve_winv, 1)

            def weight_round(m):
                dve.wait_ge(pool_wt, m + 1)
                nc.vector.tensor_scalar(wq[:, m], wnat[:, m], MAGIC + 1.0, MAGIC, ALU.min, ALU.subtract).then_inc(dve_wq, 1)

            def weight_out(i):
                dve.wait_ge(pe_wT, i + 1)
                nc.vector.tensor_scalar(wT[:].rearrange("p m n -> p (m n)")[:, I * i:I * (i + 1)],
                                        (bank7 if i % 2 == 0 else bank6).bitcast(BF16), -1.0, None, ALU.max
                                        ).then_inc(dve_wT, 1)

            def first_norm():
                dve.wait_ge(ld_x, 16 * B)
                for i in range(B * LC):
                    last = nc.vector.bn_stats(st1[:, i], xs[:, i // LC, i % LC])
                link_once(last)
                for i in range(B * LC):
                    last = nc.vector.bn_aggr(mv1[:, i], st1[:, i])
                last.then_inc(dve_stat1, 1)
                dve.wait_ge(dve_stat1, 1)
                link_once(nc.vector.tensor_scalar(ve1[:], mv1[:, :, 1], LN_EPS, None, ALU.add))

            dve.wait_ge(ld_consts, 16)
            nc.vector.tensor_copy(id16[:], id32[:])
            for i in range(3):
                k = slice(2 * DS * i, 2 * DS * (i + 1))
                last = nc.vector.tensor_copy(sel[k, :], id32[k, k])
            last.then_inc(dve_consts, 1)
            dve.wait_ge(ld_inw, 16)
            dve.wait_ge(ld_conv, 16 * 4)
            for k in range(DC):
                for h in range(HALF):
                    last = nc.vector.tensor_scalar(inwk[:, k, h], inw[:, h], cw[:, h, k:k + 1], None, ALU.mult)
            last.then_inc(dve_inwk, 1)
            weight_abs(1)
            split(0)
            dve.wait_ge(act_gate, 2)
            nc.vector.tensor_scalar(aneg[:], aneg[:], -1.0, None, ALU.mult).then_inc(dve_aneg, 1)
            dve_front_link.begin(dve, 0)
            for part in range(3):
                softplus_tail(0, dve, nc.vector, dve_front_link, part)
            scan(0)
            for k in range(B + 2):
                p, f, n = k - 2, k - 1, k + 2
                old, new, front = p >= 0, 0 <= f < B, n < B
                for s in range(STEPS):
                    g = STEPS * k + s
                    if g + 1 < B * STEPS:
                        scan(g + 1)
                    if s == 0 and new:
                        residual(f)
                    if s == 6 and new:
                        gate_times_up(f, 1)
                    if old:
                        if s == 1:
                            absmax2(p, 0)
                        if s == 2:
                            round_down(p, 0)
                        if s == 3:
                            absmax2(p, 1)
                        if s == 4:
                            round_down(p, 1)
                    if k < B:
                        times_C(g)
                    if s == 0:
                        if new:
                            stats2(f, dve_ln_link.begin(dve, f))
                        if k == 0:
                            first_norm()
                            dve.wait_ge(act_r1, 2)
                            newton(link_once, r1[:], ve1[:], nt1[:]).then_inc(dve_r1, 1)
                            norm_z(0)
                    if s == 1:
                        if new:
                            quant_tokens(f, dve_ln_link)
                        if k == 0:
                            weight_abs(2)
                            weight_means()
                    if s == 2:
                        if k == 0:
                            split(1)
                        if new:
                            tokens_out(f)
                        if old:
                            q2_out(p, 0)
                    if s == 3 and old:
                        result(p, 0)
                    if s == 4:
                        if k == 0:
                            dve_front_link.begin(dve, 1)
                            for part in range(3):
                                softplus_tail(1, dve, nc.vector, dve_front_link, part)
                        if k + 1 < B:
                            norm_z(k + 1)
                        if old:
                            q2_out(p, 1)
                    if s == 5:
                        if new:
                            gate_times_up(f, 0)
                        if old:
                            result(p, 1)
                    if s == 6 and front:
                        split(n)
                    if k == 0 and s >= 4:
                        for m in ((0, 1), (2,), (), ())[s - 4]:
                            weight_round(m)
                        for i in ((), (0, 1), (2, 3), (4, 5))[s - 4]:
                            weight_out(i)


def x_rows(t):
    return t.rearrange("b (h p) n -> b p h n", p=P)


_INS = ['x', 'ctx_1024', 'g_xattn', 'g_ffn', 'L0_xattn_in_proj_w', 'L0_xattn_conv_w', 'L0_xattn_conv_b',
        'L0_xattn_x_proj_w', 'L0_xattn_dt_proj_w', 'L0_xattn_dt_proj_b', 'L0_xattn_A_log', 'L0_xattn_D',
        'L0_ffn_w_gate', 'L0_ffn_w_up', 'L0_ffn_w_down']


def _constants():
    import numpy as np
    h = np.ones((1, 1), np.float32)
    while h.shape[0] < P:
        h = np.block([[h, h], [h, -h]])
    return {"ident": np.eye(P, dtype=np.float32), "hadamard": (h / math.sqrt(I)).astype(np.float32)}


def kernel(**inputs):
    import numpy as np
    import concourse.bacc as bacc
    from concourse.bass_utils import run_bass_kernel_spmd

    nc = bacc.Bacc("TRN2", target_bir_lowering=False, num_devices=1)
    arrays, args = {}, []
    for name, a in [(n, np.ascontiguousarray(inputs[n])) for n in _INS] + list(_constants().items()):
        arrays[f"in_{name}_dram"] = a
        args.append(nc.dram_tensor(f"in_{name}_dram", a.shape, mybir.dt.from_np(a.dtype), kind="ExternalInput").ap())
    out = nc.dram_tensor("out_0_dram", (B, L, E), F32, kind="ExternalOutput").ap()
    gated_ssm_ffn(nc, *args, out)
    return run_bass_kernel_spmd(nc, [arrays], core_ids=[0]).results[0]["out_0_dram"]
```

```python
import math
from contextlib import ExitStack

import concourse.bass as bass
from concourse import mybir

F32 = mybir.dt.float32
BF16 = mybir.dt.bfloat16
ALU = mybir.AluOpType
ACT = mybir.ActivationFunctionType
AX = mybir.AxisListType

P = 128
B, L, E = 4, 256, 256
DM, DS, DR, DC = 128, 16, 8, 4
I = 1024
HALF = E // P
LC = L // P
NI = I // P
NB = 2
STEPS = DS // NB
AHEAD = 4
RING = 4
STATES = 3
LN_EPS = 1e-5
Q_EPS = 1e-5
QB = 128.0
MAGIC = 1.5 * 2.0 ** 23
FOLDS = NI.bit_length() - 1
DT0 = 96


class Chain:

    def __init__(self, sem, per_batch):
        self.sem, self.per_batch = sem, per_batch

    def begin(self, eng, batch):
        self.eng, self.base, self.count = eng, batch * self.per_batch, 0
        return self

    def __call__(self, ins):
        self.count += 1
        ins.then_inc(self.sem, 1)
        self.eng.wait_ge(self.sem, self.base + self.count)

    def end(self):
        assert self.count == self.per_batch, (self.count, self.per_batch)


def gated_ssm_ffn(nc, x, ctx_1024, g_xattn, g_ffn, in_proj_w, conv_w, conv_b, x_proj_w, dt_proj_w, dt_proj_b,
                  A_log, D, w_gate, w_up, w_down, ident, hadamard, out):
    stack = ExitStack()
    with stack:
        def sb(name, shape, dt=F32):
            return stack.enter_context(nc.sbuf_tensor(name, shape, dt))

        def sem(name):
            return stack.enter_context(nc.semaphore(name))

        xs = sb("xs", [P, B, LC, E])
        ctxs = sb("ctxs", [P, B, LC, DM])
        ctxT = sb("ctxT", [DM, B, L])
        id32 = sb("id32", [P, P])
        id16 = sb("id16", [P, P], BF16)
        had = sb("had", [P, P])
        sel = sb("sel", [3 * 2 * DS, 2 * DS], BF16)
        inw = sb("inw", [P, HALF, DM])
        inwk = sb("inwk", [P, DC, HALF, DM])
        inwT = sb("inwT", [DM, DC, E])
        xpw = sb("xpw", [DR + 2 * DS, E])
        xpwT = sb("xpwT", [P, HALF, DT0 + DR])
        dtw = sb("dtw", [P, HALF, DT0 + DR])
        dtwT = sb("dtwT", [DT0 + DR, E])
        cw = sb("cw", [P, HALF, DC])
        cb = sb("cb", [P, HALF])
        dtb = sb("dtb", [P, HALF])
        dskip = sb("dskip", [P, HALF])
        alog = sb("alog", [P, HALF, DS])
        aneg = sb("aneg", [P, HALF, DS])
        gates = sb("gates", [P, 2])
        tg = sb("tg", [P, 2])
        onesf = sb("onesf", [P, P])
        eps_c = sb("eps_c", [P, 1])
        one_c = sb("one_c", [P, 1])
        magic_c = sb("magic_c", [P, 1])
        zero_c = sb("zero_c", [P, 1])
        st1 = sb("st1", [P, B * LC, 6])
        mv1 = sb("mv1", [P, B * LC, 2])
        ln1 = sb("ln1", [P, B * LC])
        r1 = sb("r1", [P, B * LC])
        nt1 = sb("nt1", [P, B * LC])
        ve1 = sb("ve1", [P, B * LC])
        zn = sb("zn", [P, HALF, L])
        sz = sb("sz", [P, HALF, L])
        szT = sb("szT", [P, LC, E])
        conv = sb("conv", [P, HALF, L])
        u = sb("u", [P, 2, HALF, L])
        bc3 = sb("bc3", [3 * 2 * DS, B, L], BF16)
        res1 = sb("res1", [3 * 2 * DS, L])
        mid = sb("mid", [3 * 2 * DS, L], BF16)
        dtlo = sb("dtlo", [DT0 + DR, L])
        spa = sb("spa", [P, HALF, L])
        spe = sb("spe", [P, HALF, L])
        spl = sb("spl", [P, HALF, L])
        spr = sb("spr", [P, HALF, L])
        spm = spa
        delta = sb("delta", [P, 2, HALF, L])
        du = sb("du", [P, 2, HALF, L])
        skip = sb("skip", [P, 2, HALF, L])
        Bs = sb("Bs", [P, RING, NB, L])
        decay = sb("decay", [P, RING, HALF, NB, L])
        drive = sb("drive", [P, RING, HALF, NB, L])
        state = sb("state", [P, STATES, HALF, NB, L])
        prod = sb("prod", [P, RING, HALF, NB, L])
        x2 = sb("x2", [P, 2, LC, E])
        st2 = sb("st2", [P, LC, 6])
        mv2 = sb("mv2", [P, LC, 2])
        ve2 = sb("ve2", [P, LC])
        ln2 = sb("ln2", [P, LC])
        r2 = sb("r2", [P, LC])
        nt2 = sb("nt2", [P, LC])
        xn = sb("xn", [P, LC, E])
        yg = xn
        amax = sb("amax", [P, LC])
        ainv = sb("ainv", [P, LC])
        gs = sb("gs", [P, LC])
        us = sb("us", [P, LC])
        q = sb("q", [P, LC, E], BF16)
        qT = sb("qT", [P, HALF, L], BF16)
        wnat = sb("wnat", [P, 3, 2 * I])
        wq = sb("wq", [P, 3, 2 * I], BF16)
        wT = sb("wT", [P, 3, 2 * I], BF16)
        hT = sb("hT", [P, LC, NI, P])
        wabs = hT[:].rearrange("p t a c -> p (t a c)")
        wsum = sb("wsum", [P, 3])
        wmean = sb("wmean", [P, 3])
        winv = sb("winv", [P, 3])
        wdn = sb("wdn", [P, 1])
        inter = wnat[:, 0].rearrange("p (t n) -> p t n", t=LC)
        had2 = wnat[:, 2, 0:4 * P].rearrange("p (j i c) -> p j i c", j=2, i=2)
        fold = wnat[:, 1].rearrange("p (t n) -> p t n", t=LC)
        sg = wq[:, 0:2].rearrange("p m n -> p (m n)").bitcast(F32).rearrange("p (t n) -> p t n", t=LC)
        am2 = sb("am2", [P, LC])
        sc2 = sb("sc2", [P, LC])
        dq2 = sb("dq2", [P, LC])
        tq = ctxs[:].rearrange("p b c d -> p (b c d)")
        q2 = wq[:, 2].rearrange("p (t n) -> p t n", t=LC)
        q2T = sb("q2T", [P, LC, NI, P], BF16)
        ot = sb("ot", [P, LC, E])

        BC, GP, UP = (stack.enter_context(nc.psum_tensor(n, [P, 2 * 512], F32)) for n in ("BC", "GP", "UP"))
        PB, PC = BC[:, 0:512], BC[:, 512:1024]
        PY = stack.enter_context(nc.psum_tensor("PY", [P, 512], F32))
        X = stack.enter_context(nc.psum_tensor("X", [P, 512], F32))[:]
        bank4, bank5 = GP[:, 0:512], GP[:, 512:1024]
        bank6, bank7 = UP[:, 0:512], UP[:, 512:1024]

        wgT = wT[:, 0].rearrange("p (h i) -> p h i", h=HALF)
        wuT = wT[:, 1].rearrange("p (h i) -> p h i", h=HALF)
        wdT = wT[:, 2].rearrange("p (a o) -> p a o", a=NI)

        ld_consts, ld_ctx0, ld_inw, ld_taps, ld_small, ld_ctx, ld_x, ld_had, ld_gate = (
            sem(n) for n in ("ld_consts", "ld_ctx0", "ld_inw", "ld_taps", "ld_small", "ld_ctx", "ld_x", "ld_had",
                             "ld_gate"))
        ld_conv, ld_w = sem("ld_conv"), [sem(f"ld_w{i}") for i in range(3)]
        zeroed, consts, decay_zeroed = sem("zeroed"), sem("consts"), sem("decay_zeroed")
        pe_setup, act_setup, dve_setup = sem("pe_setup"), sem("act_setup"), sem("dve_setup")
        act_gate, dve_aneg, dve_consts = sem("act_gate"), sem("dve_aneg"), sem("dve_consts")
        dve_stat1, act_r1, dve_r1 = sem("dve_stat1"), sem("act_r1"), sem("dve_r1")
        wabs_done, pe_wsum, dve_winv, pool_wt, dve_wq, pe_wT, dve_wT = (
            sem(n) for n in ("wabs_done", "pe_wsum", "dve_winv", "pool_wt", "dve_wq", "pe_wT", "dve_wT"))
        pe_B, act_B, act_decay, pool_drive, dve_scan, pe_C, dve_prod, pe_acc = (
            sem(n) for n in ("pe_B", "act_B", "act_decay", "pool_drive", "dve_scan", "pe_C", "dve_prod", "pe_acc"))
        pe_xin, dve_inwk, act_conv, act_u, pe_xdbl, dve_split, act_dtlo, pe_draw = (
            sem(n) for n in ("pe_xin", "dve_inwk", "act_conv", "act_u", "pe_xdbl", "dve_split", "act_dtlo", "pe_draw"))
        act_spread, act_sp, delta_ready, du_ready, dve_zn, act_sz, pe_szT, act_szT, pe_y, dve_x2 = (
            sem(n) for n in ("act_spread", "act_sp", "delta_ready", "du_ready", "dve_zn", "act_sz", "pe_szT", "act_szT",
                             "pe_y", "dve_x2"))
        dve_stat2, act_r2, dve_q, pe_qT, dve_qT, pe_gate, pe_up, act_sg, dve_mul = (
            sem(n) for n in ("dve_stat2", "act_r2", "dve_q", "pe_qT", "dve_qT", "pe_gate", "pe_up", "act_sg", "dve_mul"))
        pool_fold, pe_tp, act_tp, pe_h, dve_sc, act_tq, dve_q2, pe_q2T, dve_q2T, pe_dn, dve_out = (
            sem(n) for n in ("pool_fold", "pe_tp", "act_tp", "pe_h", "dve_sc", "act_tq", "dve_q2", "pe_q2T", "dve_q2T",
                             "pe_dn", "dve_out"))
        skip_ready = sem("skip_ready")
        stored = [sem(f"stored_{t}") for t in range(LC)]
        pool_front_link = Chain(sem("pool_front_link"), 4)
        dve_front_link = Chain(sem("dve_front_link"), 4)
        had_built, dve_fold = sem("had_built"), sem("dve_fold")
        dve_once = sem("dve_once")
        act_r2_link = Chain(sem("act_r2_link"), 1)
        act_sp_link = Chain(sem("act_sp_link"), 1)
        pool_stage = sem("pool_stage")
        dve_split_link = Chain(sem("dve_split_link"), 3)
        dve_gs, dve_dq = sem("dve_gs"), sem("dve_dq")
        dve_ln_link = Chain(sem("dve_ln_link"), 11)
        dve_sc_link = Chain(sem("dve_sc_link"), 2)

        block = stack.enter_context(nc.Block())

        def front_bank(n):
            return bank4 if n < 2 else X

        def transform_bank(f, t):
            return BC if (f, t) in ((B - 2, 1), (B - 1, 0)) else UP

        def q2_bank(f, t):
            return (bank4 if t == 0 else X) if f < B - 2 else (X if (f, t) == (B - 1, 1) else PY[:])

        def down_bank(f, t):
            return bank5 if f < B - 2 and t == 0 else q2_bank(f, t)

        def softplus_tail(n, eng, ops, link, part):
            if part == 0:
                eng.wait_ge(act_sp, n + 1)
                link(ops.tensor_scalar(spm[:], spe[:], 1.0, 1.0, ALU.mult, ALU.add))
                link(ops.tensor_scalar(spm[:], spm[:], 1.0, -1.0, ALU.mult, ALU.add))
                link(ops.tensor_tensor(spm[:], spm[:], spe[:], ALU.subtract))
            if part == 1:
                if n >= 2:
                    eng.wait_ge(act_decay, STEPS * (n - 1))
                link(ops.tensor_tensor(spl[:], spl[:], spm[:], ALU.subtract))
                ops.tensor_tensor(delta[:, n % 2], spl[:], spr[:], ALU.add).then_inc(delta_ready, 1)
            if part == 2:
                if n >= 2:
                    eng.wait_ge(pe_y, n - 1)
                    eng.wait_ge(pool_drive, STEPS * (n - 1))
                eng.wait_ge(delta_ready, n + 1)
                ops.tensor_tensor(du[:, n % 2], delta[:, n % 2], u[:, n % 2], ALU.mult).then_inc(du_ready, 1)
                for h in range(HALF):
                    last = ops.tensor_scalar(skip[:, n % 2, h], u[:, n % 2, h], dskip[:, h:h + 1], 1.0,
                                             ALU.mult, ALU.mult)
                last.then_inc(skip_ready, 1)
                link.end()

        @block.sync
        def _(sp):
            cr = tiles(ctx_1024)
            sp.dma_start(ctxs[:, 0], cr[:, 0:LC]).then_inc(ld_ctx0, 16)
            sp.dma_start(inw[:], in_proj_w.rearrange("(h p) d -> p h d", p=P)).then_inc(ld_inw, 16)
            sp.dma_start(xpw[:], x_proj_w).then_inc(ld_small, 16)
            sp.wait_ge(zeroed, 1)
            sp.dma_start(dtw[:, :, DT0:DT0 + DR], dt_proj_w.rearrange("(h p) r -> p h r", p=P)).then_inc(ld_small, 16)
            sp.dma_start(ctxs[:, 1:B].rearrange("p b c d -> p (b c) d"), cr[:, LC:B * LC]).then_inc(ld_ctx, 16)
            sp.dma_start(wnat[:, 0].rearrange("p (a h) -> p a h", a=NI),
                         w_gate.rearrange("(a p) h -> p a h", p=P)).then_inc(ld_w[0], 16)
            sp.dma_start(xs[:].rearrange("p b c d -> p (b c) d"), tiles(x)).then_inc(ld_x, 16)
            sp.dma_start(wnat[:, 1].rearrange("p (a h) -> p a h", a=NI),
                         w_up.rearrange("(a p) h -> p a h", p=P)).then_inc(ld_w[1], 16)
            sp.dma_start(wnat[:, 2].rearrange("p (o i) -> p o i", o=HALF),
                         w_down.rearrange("(o p) i -> p o i", p=P)).then_inc(ld_w[2], 16)
            sp.dma_start(had[:], hadamard).then_inc(ld_had, 16)
            for b in range(B):
                for t in range(LC):
                    sp.wait_ge(dve_out, LC * b + t + 1)
                    sp.dma_start(tiles(out)[:, LC * b + t], ot[:, t]).then_inc(stored[t], 16)
            for t in range(LC):
                sp.wait_ge(stored[t], 16 * B)

        @block.tensor
        def _(pe):
            def setup():
                pe.wait_ge(ld_consts, 16)
                pe.wait_ge(ld_ctx0, 16)
                for c in range(LC):
                    last = nc.tensor.transpose(bank4[:, P * c:P * (c + 1)], ctxs[:, 0, c], id32[:])
                last.then_inc(pe_setup, 1)
                pe.wait_ge(dve_inwk, 2)
                for k in range(DC):
                    for h in range(HALF):
                        last = nc.tensor.transpose(UP[:, E * k + P * h:E * k + P * (h + 1)], inwk[:, k, h], id32[:])
                last.then_inc(pe_setup, 1)
                pe.wait_ge(ld_small, 16 * 2)
                for h in range(HALF):
                    last = nc.tensor.transpose(bank5[:, P * h:P * h + DR + 2 * DS], xpw[:, P * h:P * (h + 1)],
                                               id32[0:DR + 2 * DS, 0:DR + 2 * DS])
                last.then_inc(pe_setup, 1)
                for h in range(HALF):
                    last = nc.tensor.transpose(PB[0:DT0 + DR, P * h:P * (h + 1)], dtw[:, h], id32[:])
                last.then_inc(pe_setup, 1)

            def setup_late():
                pe.wait_ge(ld_ctx, 16)
                for b in range(1, B):
                    for c in range(LC):
                        at = (b - 1) * L + P * c
                        last = nc.tensor.transpose((PC if at < 512 else PY)[:, at % 512:at % 512 + P], ctxs[:, b, c], id32[:])
                last.then_inc(pe_setup, 1)

            def B_rows(m):
                b, j = divmod(m, STEPS)
                pe.wait_ge(dve_split, b + 1)
                if m >= 1:
                    pe.wait_ge(act_B, m)
                else:
                    pe.wait_ge(act_setup, 4)
                for n in range(NB):
                    last = nc.tensor.matmul(PB[:, L * n:L * (n + 1)], row_pick(NB * j + n), bc3[:, b, :],
                                            start=True, stop=True)
                last.then_inc(pe_B, 1)

            def C_rows(m):
                b, j = divmod(m, STEPS)
                pe.wait_ge(dve_split, b + 1)
                if m >= 1:
                    pe.wait_ge(dve_prod, m)
                else:
                    pe.wait_ge(act_setup, 5)
                for n in range(NB):
                    last = nc.tensor.matmul(PC[:, L * n:L * (n + 1)], row_pick(DS + NB * j + n), bc3[:, b, :],
                                            start=True, stop=True)
                last.then_inc(pe_C, 1)

            def row_pick(r):
                return sel[:, r:r + 1].to_broadcast([3 * 2 * DS, P])

            def accumulate(g):
                b, j = divmod(g, STEPS)
                pe.wait_ge(dve_prod, g + 1)
                if j == 0 and b >= 1:
                    pe.wait_ge(dve_x2, b)
                for h in range(HALF):
                    for n in range(NB):
                        for c in range(LC):
                            last = nc.tensor.matmul(PY[:, E * c + P * h:E * c + P * (h + 1)],
                                                    prod[:, g % RING, h, n, P * c:P * (c + 1)], id32[:],
                                                    is_transpose=True, start=(j == 0 and h == n == c == 0), stop=False,
                                                    skip_group_check=True)
                last.then_inc(pe_acc, 1)
                if j == STEPS - 1:
                    pe.wait_ge(skip_ready, b + 1)
                    for h in range(HALF):
                        for c in range(LC):
                            last = nc.tensor.matmul(PY[:, E * c + P * h:E * c + P * (h + 1)],
                                                    skip[:, b % 2, h, P * c:P * (c + 1)], id32[:],
                                                    is_transpose=True, start=False, stop=(h == HALF - 1 and c == LC - 1),
                                                    skip_group_check=True)
                    last.then_inc(pe_y, 1)

            def in_proj(n):
                if n == 0:
                    pe.wait_ge(act_setup, 2)
                elif n == 1:
                    pe.wait_ge(act_setup, 5)
                    pe.wait_ge(act_spread, n)
                elif n == 2:
                    pass
                else:
                    pe.wait_ge(dve_qT, n - 2)
                for h in range(HALF):
                    for d in range(DC):
                        last = nc.tensor.matmul(front_bank(n)[:, L * h + d:L * (h + 1)],
                                                inwT[:, DC - 1 - d, P * h:P * (h + 1)], ctxT[:, n, 0:L - d],
                                                start=(d == 0), stop=(d == DC - 1))
                last.then_inc(pe_xin, 1)

            def x_dbl(n):
                pe.wait_ge(act_u, n + 1)
                if n == 0:
                    pe.wait_ge(act_setup, 3)
                if n >= 2:
                    pe.wait_ge(act_conv, n - 1)
                if n >= 4:
                    pe.wait_ge(dve_out, LC * (n - 3))
                for h in range(HALF):
                    last = nc.tensor.matmul(front_bank(n)[0:DT0 + DR, 0:L], xpwT[:, h, :], u[:, n % 2, h, :],
                                            start=(h == 0), stop=(h == HALF - 1))
                last.then_inc(pe_xdbl, 1)

            def dt_proj(n):
                pe.wait_ge(act_dtlo, n + 1)
                pe.wait_ge(dve_split, n + 1)
                if n == 0:
                    pe.wait_ge(act_setup, 4)
                for h in range(HALF):
                    last = nc.tensor.matmul(front_bank(n)[:, L * h:L * (h + 1)], dtwT[DT0:DT0 + DR, P * h:P * (h + 1)],
                                            dtlo[DT0:DT0 + DR, :], start=True, stop=True)
                last.then_inc(pe_draw, 1)

            def gate_T(k):
                pe.wait_ge(act_sz, k + 1)
                if k >= 1 and k + 1 < B:
                    pe.wait_ge(act_spread, k + 2)
                if k + 1 == B:
                    pe.wait_ge(dve_out, LC * (k - 2))
                for h in range(HALF):
                    for c in range(LC):
                        last = nc.tensor.transpose((bank5 if k == 0 else X)[:, E * c + P * h:E * c + P * (h + 1)],
                                                   sz[:, h, P * c:P * (c + 1)], id32[:])
                last.then_inc(pe_szT, 1)

            def tokens_T(f):
                pe.wait_ge(dve_q, f + 1)
                if f + 1 < B:
                    pe.wait_ge(act_szT, f + 2)
                else:
                    pe.wait_ge(dve_out, LC * (f - 1))
                for c in range(LC):
                    for h in range(HALF):
                        last = nc.tensor.transpose(X.bitcast(BF16)[:, L * h + P * c:L * h + P * (c + 1)],
                                                   q[:, c, P * h:P * (h + 1)], id16[:])
                last.then_inc(pe_qT, 1)

            def gate(f, t):
                pe.wait_ge(dve_qT, f + 1)
                if f == 0 and t == 0:
                    pe.wait_ge(dve_wT, 6)
                    pe.wait_ge(act_spread, 2)
                    pe.wait_ge(act_szT, 1)
                elif t == 0 and f < B - 1:
                    pe.wait_ge(dve_out, LC * (f - 1) + 1)
                elif t == 0:
                    pe.wait_ge(act_tp, LC * f)
                elif 0 < f < B - 1:
                    pe.wait_ge(act_tq, LC * f)
                elif f == B - 1:
                    pe.wait_ge(act_tq, LC * f - 1)
                tokens_by(f, t, wgT, pe_gate)

            def up(f, t):
                pe.wait_ge(act_sg, LC * f + t + 1)
                tokens_by(f, t, wuT, pe_up)

            def tokens_by(f, t, w, done):
                for i in range(2):
                    for h in range(HALF):
                        last = nc.tensor.matmul((GP, UP)[t][:, 512 * i:512 * (i + 1)], qT[:, h, P * t:P * (t + 1)],
                                                w[:, h, 512 * i:512 * (i + 1)],
                                                start=(h == 0), stop=(h == HALF - 1))
                last.then_inc(done, 1)

            def inter_T(f, t):
                if f < B - 1:
                    pe.wait_ge(pool_fold, LC * f + t + 1)
                else:
                    pe.wait_ge(dve_fold, FOLDS * (t + 1))
                if t == 1:
                    pe.wait_ge(act_tp, LC * f + 1)
                src = inter if f < B - 1 else fold
                for a in range(NI):
                    last = nc.tensor.transpose(GP[:, P * a:P * (a + 1)], src[:, t, P * a:P * (a + 1)], id32[:])
                last.then_inc(pe_tp, 1)

            def hadamard_mm(f, t):
                pe.wait_ge(act_tp, LC * f + t + 1)
                if f == t == 0:
                    pe.wait_ge(had_built, 1)
                if (f, t) == (B - 2, 1):
                    pe.wait_ge(act_B, B * STEPS)
                    pe.wait_ge(dve_prod, B * STEPS)
                elif (f, t) == (B - 1, 0):
                    pe.wait_ge(act_tq, LC * f)
                elif f == B - 1:
                    pe.wait_ge(dve_mul, LC * f + 2)
                elif t == 0:
                    pe.wait_ge(dve_mul, LC * f + 2)
                else:
                    pe.wait_ge(act_tq, LC * f + 1)
                dst = transform_bank(f, t)
                for a in range(NI):
                    if f < B - 1:
                        last = nc.tensor.matmul(dst[:, E * (a // 2):E * (a // 2 + 1)], hT[:, t, a, :],
                                                had2[:, a % 2].rearrange("p i c -> p (i c)"),
                                                start=(a % 2 == 0), stop=(a % 2 == 1))
                    else:
                        last = nc.tensor.matmul(dst[:, P * a:P * (a + 1)], hT[:, t, a, :], had2[:, 0, 0],
                                                start=True, stop=True)
                last.then_inc(pe_h, 1)

            def q2_T(f, t):
                pe.wait_ge(dve_q2, LC * f + t + 1)
                if f < B - 2 and t == 0:
                    pe.wait_ge(act_tp, LC * f + 2)
                elif f < B - 2:
                    pe.wait_ge(dve_qT, f + 2)
                    if f + 4 < B:
                        pe.wait_ge(act_conv, f + 3)
                elif (f, t) == (B - 2, 0):
                    pe.wait_ge(dve_x2, B)
                elif (f, t) != (B - 1, 1):
                    pe.wait_ge(dve_out, LC * f + t)
                else:
                    pe.wait_ge(dve_qT, B)
                for a in range(NI):
                    last = nc.tensor.transpose(q2_bank(f, t).bitcast(BF16)[:, P * a:P * (a + 1)],
                                               q2[:, t, P * a:P * (a + 1)], id16[:])
                last.then_inc(pe_q2T, 1)

            def down(f, t):
                pe.wait_ge(dve_q2T, LC * f + t + 1)
                for a in range(NI):
                    last = nc.tensor.matmul(down_bank(f, t)[:, 0:E], q2T[:, t, a, :], wdT[:, a, :],
                                            start=(a == 0), stop=(a == NI - 1))
                last.then_inc(pe_dn, 1)

            def weight_sum():
                pe.wait_ge(wabs_done, 3)
                pe.wait_ge(act_setup, 2)
                nc.tensor.matmul(bank7[:, 0:3], onesf[:], wsum[:], start=True, stop=True).then_inc(pe_wsum, 1)

            def weight_T(i):
                m, part = divmod(i, 2)
                pe.wait_ge(dve_wq, m + 1)
                if i == 0:
                    pe.wait_ge(dve_winv, 1)
                if i >= 2:
                    pe.wait_ge(dve_wT, i - 1)
                bk = (bank7 if i % 2 == 0 else bank6).bitcast(BF16)
                for k in range(8):
                    if m < 2:
                        blk = wq[:, m].rearrange("p (a h c) -> p h a c", a=NI, h=HALF)[:, part, k, :]
                    else:
                        a, oh = 4 * part + k // 2, k % 2
                        blk = wq[:, m].rearrange("p (o a c) -> p o a c", o=HALF, a=NI)[:, oh, a, :]
                    last = nc.tensor.transpose(bk[:, P * k:P * (k + 1)], blk, id16[:])
                last.then_inc(pe_wT, 1)

            setup()
            in_proj(0)
            pe.wait_ge(dve_consts, 1)
            x_dbl(0)
            dt_proj(0)
            B_rows(0)
            setup_late()
            B_rows(1)
            in_proj(1)
            C_rows(0)
            for m in range(2, AHEAD):
                B_rows(m)
            for k in range(B):
                p, f, n = k - 2, k - 1, k + 2
                old, new, front = p >= 0, f >= 0, n < B
                for s in range(STEPS):
                    g = STEPS * k + s
                    if g + AHEAD < B * STEPS:
                        B_rows(g + AHEAD)
                    if s == 0 and old:
                        hadamard_mm(p, 0)
                    if s == 1:
                        if k >= 1:
                            gate_T(k)
                        if old:
                            inter_T(p, 1)
                        if k == 0:
                            x_dbl(1)
                    if s == 2:
                        if new:
                            tokens_T(f)
                        if old:
                            hadamard_mm(p, 1)
                            q2_T(p, 0)
                        if k == 0:
                            dt_proj(1)
                            weight_sum()
                            gate_T(0)
                    if s == 3:
                        if old:
                            down(p, 0)
                        if front:
                            in_proj(n)
                    if s == 4:
                        if new:
                            gate(f, 0)
                            gate(f, 1)
                        if old:
                            q2_T(p, 1)
                    if s == 5 and old:
                        down(p, 1)
                    if s == 6 and front:
                        x_dbl(n)
                    if s == 7:
                        if front:
                            dt_proj(n)
                        if new:
                            inter_T(f, 0)
                    if k == 0 and s >= 4:
                        for i in ((0, 1), (2,), (3, 4), (5,))[s - 4]:
                            weight_T(i)
                    if g + 1 < B * STEPS:
                        C_rows(g + 1)
                    accumulate(g)
                    if s == 5 and new:
                        up(f, 0)
                        up(f, 1)
            p, f = B - 2, B - 1
            hadamard_mm(p, 0)
            inter_T(p, 1)
            hadamard_mm(p, 1)
            tokens_T(f)
            gate(f, 0)
            gate(f, 1)
            q2_T(p, 0)
            down(p, 0)
            up(f, 0)
            up(f, 1)
            q2_T(p, 1)
            down(p, 1)
            for t in range(LC):
                inter_T(f, t)
                hadamard_mm(f, t)
            for t in range(LC):
                q2_T(f, t)
                down(f, t)

        @block.scalar
        def _(act):
            def setup_loads():
                act.dma_start(id32[:], ident).then_inc(ld_consts, 16)
                act.dma_start(cw[:], conv_w.rearrange("(h p) k -> p h k", p=P)).then_inc(ld_taps, 16)

            def small_loads():
                for dst, src in ((cb, conv_b), (dtb, dt_proj_b), (dskip, D)):
                    with nc.allow_non_contiguous_dma(reason="one value per partition"):
                        act.dma_start(dst[:], src.rearrange("(h p) -> p h", p=P)).then_inc(ld_conv, 16)
                act.dma_start(alog[:], A_log.rearrange("(h p) n -> p h n", p=P)).then_inc(ld_gate, 16)
                act.dma_start(gates[:, 0:1], g_xattn.partition_broadcast(P)).then_inc(ld_gate, 16)
                act.dma_start(gates[:, 1:2], g_ffn.partition_broadcast(P)).then_inc(ld_gate, 16)

            def copy_B(m):
                act.wait_ge(pe_B, m + 1)
                if m >= RING:
                    act.wait_ge(pool_drive, m - RING + 1)
                nc.scalar.copy(Bs[:, m % RING], PB.rearrange("p (n l) -> p n l", n=NB)).then_inc(act_B, 1)

            def decays(m):
                b, j = divmod(m, STEPS)
                act.wait_ge(delta_ready, b + 1)
                if m >= RING:
                    act.wait_ge(dve_scan, m - RING + 1)
                for h in range(HALF):
                    for n in range(NB):
                        last = nc.scalar.activation(decay[:, m % RING, h, n, 1:L], delta[:, b % 2, h, 1:L], ACT.Exp,
                                                    bias=zero_c[:], scale=aneg[:, h, NB * j + n:NB * j + n + 1])
                last.then_inc(act_decay, 1)

            def conv_out(n):
                act.wait_ge(pe_xin, n + 1)
                if n >= 3:
                    act.wait_ge(act_u, n)
                for h in range(HALF):
                    last = nc.scalar.activation(conv[:, h, :], X[:, L * h:L * (h + 1)], ACT.Identity, bias=cb[:, h:h + 1])
                last.then_inc(act_conv, 1)

            def silu_u(n):
                if n < 2:
                    act.wait_ge(pe_xin, n + 1)
                    for h in range(HALF):
                        last = nc.scalar.activation(u[:, n, h], bank4[:, L * h:L * (h + 1)], ACT.Silu, bias=cb[:, h:h + 1])
                    last.then_inc(act_u, 1)
                else:
                    act.wait_ge(act_conv, n - 1)
                    act.wait_ge(pe_xdbl, n - 1)
                    act.wait_ge(skip_ready, n - 1)
                    nc.scalar.activation(u[:, n % 2], conv[:], ACT.Silu, bias=zero_c[:]).then_inc(act_u, 1)

            def silu_z(n):
                act.wait_ge(dve_zn, n + 1)
                if n >= 1:
                    act.wait_ge(pe_szT, n)
                nc.scalar.activation(sz[:], zn[:], ACT.Silu, bias=zero_c[:]).then_inc(act_sz, 1)

            def dt_rows(n):
                act.wait_ge(pe_xdbl, n + 1)
                nc.scalar.copy(dtlo[DT0:DT0 + DR, :], front_bank(n)[DT0:DT0 + DR, 0:L]).then_inc(act_dtlo, 1)

            def softplus(n):
                link = act_sp_link.begin(act, n)
                act.wait_ge(pe_draw, n + 1)
                if n >= 1:
                    act.wait_ge(delta_ready, n)
                for h in range(HALF):
                    v = front_bank(n)[:, L * h:L * (h + 1)]
                    nc.scalar.activation(spr[:, h], v, ACT.Relu, bias=dtb[:, h:h + 1])
                    last = nc.scalar.activation(spa[:, h], v, ACT.Abs, bias=dtb[:, h:h + 1])
                last.then_inc(act_spread, 1)
                act.wait_ge(act_spread, n + 1)
                link(nc.scalar.activation(spe[:], spa[:], ACT.Exp, bias=zero_c[:], scale=-1.0))
                nc.scalar.activation(spl[:], spe[:], ACT.Ln, bias=one_c[:]).then_inc(act_sp, 1)
                link.end()

            def gate_out(k):
                act.wait_ge(pe_szT, k + 1)
                if k >= 1:
                    act.wait_ge(dve_x2, k)
                nc.scalar.activation(szT[:], (bank5 if k == 0 else X).rearrange("p (c e) -> p c e", c=LC), ACT.Copy,
                                     scale=tg[:, 0:1]).then_inc(act_szT, 1)

            def rstd2(f):
                link = act_r2_link.begin(act, f)
                act.wait_ge(dve_stat2, f + 1)
                link(nc.scalar.activation(ln2[:], mv2[:, :, 1], ACT.Ln, bias=eps_c[:]))
                nc.scalar.activation(r2[:], ln2[:], ACT.Exp, bias=zero_c[:], scale=-0.5).then_inc(act_r2, 1)
                link.end()

            def silu_gate(f, t):
                act.wait_ge(pe_gate, LC * f + t + 1)
                act.wait_ge(dve_gs, f + 1)
                nc.scalar.activation(sg[:, t], (GP, UP)[t][:], ACT.Silu, bias=zero_c[:], scale=gs[:, t:t + 1]).then_inc(act_sg, 1)

            def inter_out(f, t):
                act.wait_ge(pe_tp, LC * f + t + 1)
                nc.scalar.copy(hT[:, t].rearrange("p a c -> p (a c)"), GP[:]).then_inc(act_tp, 1)

            def quant_down(f, t):
                act.wait_ge(dve_sc, LC * f + t + 1)
                if LC * f + t >= 1:
                    act.wait_ge(dve_q2, LC * f + t)
                nc.scalar.activation(tq, transform_bank(f, t)[:], ACT.Identity, bias=magic_c[:], scale=sc2[:, t:t + 1]
                                     ).then_inc(act_tq, 1)

            def weight_abs(m):
                act.wait_ge(ld_w[m], 16)
                if m == 2:
                    act.wait_ge(wabs_done, 1)
                nc.scalar.activation(wabs, wnat[:, m], ACT.Abs, bias=zero_c[:],
                                     accum_out=wsum[:, m:m + 1]).then_inc(wabs_done, 1)

            def for_silu():
                nc.scalar.preload_act_table_set("silu_and_others")

            def for_exp():
                nc.scalar.preload_act_table_set("natural_log_exp_and_others")

            setup_loads()
            for_silu()
            small_loads()
            act.wait_ge(consts, 1)
            act.wait_ge(pe_setup, 1)
            nc.scalar.copy(ctxT[:, 0], bank4[:, 0:L]).then_inc(act_setup, 1)
            act.wait_ge(pe_setup, 2)
            nc.scalar.copy(inwT[:].rearrange("p k e -> p (k e)"), UP[:]).then_inc(act_setup, 1)
            act.wait_ge(pe_setup, 3)
            xp = bank5[:, 0:HALF * P].rearrange("p (h k) -> p h k", h=HALF)
            nc.scalar.copy(xpwT[:, :, 0:DT0].rearrange("p h (i k) -> p h i k", i=3),
                           xp[:, :, DR:DR + 2 * DS].unsqueeze(2).to_broadcast([P, HALF, 3, 2 * DS]))
            nc.scalar.copy(xpwT[:, :, DT0:DT0 + DR], xp[:, :, 0:DR]).then_inc(act_setup, 1)
            act.wait_ge(pe_setup, 4)
            nc.scalar.copy(dtwT[DT0:DT0 + DR, :], PB[DT0:DT0 + DR, 0:E]).then_inc(act_setup, 1)
            act.wait_ge(ld_gate, 16 * 3)
            nc.scalar.activation(tg[:], gates[:], ACT.Tanh, bias=zero_c[:]).then_inc(act_gate, 1)
            act.wait_ge(ld_conv, 16 * 3)
            silu_u(0)
            for_exp()
            nc.scalar.activation(aneg[:], alog[:], ACT.Exp, bias=zero_c[:]).then_inc(act_gate, 1)
            dt_rows(0)
            softplus(0)
            copy_B(0)
            act.wait_ge(pe_setup, 5)
            nc.scalar.copy(ctxT[:, 1:3], PC.rearrange("p (b l) -> p b l", b=2))
            nc.scalar.copy(ctxT[:, 3], PY[:, 0:L]).then_inc(act_setup, 1)
            act.wait_ge(dve_aneg, 1)
            act.wait_ge(decay_zeroed, 1)
            decays(0)
            for m in range(1, AHEAD):
                copy_B(m)
                decays(m)
            for k in range(B):
                p, f, n = k - 2, k - 1, k + 2
                old, new, front = p >= 0, f >= 0, n < B
                for s in range(STEPS):
                    g = STEPS * k + s
                    if k == 0 and s == 0:
                        act.wait_ge(dve_stat1, 1)
                        nc.scalar.activation(ln1[:], mv1[:, :, 1], ACT.Ln, bias=eps_c[:]).then_inc(act_r1, 1)
                        act.wait_ge(act_r1, 1)
                        nc.scalar.activation(r1[:], ln1[:], ACT.Exp, bias=zero_c[:], scale=-0.5).then_inc(act_r1, 1)
                    if g + AHEAD < B * STEPS:
                        copy_B(g + AHEAD)
                        decays(g + AHEAD)
                    if s == 0:
                        if new:
                            rstd2(f)
                        if k == 0:
                            for_silu()
                            silu_u(1)
                            silu_z(0)
                            for_exp()
                    if s == 1:
                        if k >= 1:
                            gate_out(k)
                        if old:
                            inter_out(p, 1)
                            quant_down(p, 0)
                        if k == 0:
                            dt_rows(1)
                            weight_abs(0)
                    if s == 2 and k == 0:
                        softplus(1)
                        gate_out(0)
                    if s == 3:
                        if front:
                            conv_out(n)
                        if old:
                            quant_down(p, 1)
                    if s == 4:
                        if new or k + 1 < B:
                            for_silu()
                        if new:
                            silu_gate(f, 0)
                        if front:
                            silu_u(n)
                        if k + 1 < B:
                            silu_z(k + 1)
                        if new:
                            silu_gate(f, 1)
                        for_exp()
                    if s == 6 and front:
                        dt_rows(n)
                    if s == 7:
                        if new:
                            inter_out(f, 0)
                        if front:
                            softplus(n)
            p, f = B - 2, B - 1
            rstd2(f)
            inter_out(p, 1)
            quant_down(p, 0)
            for_silu()
            quant_down(p, 1)
            silu_gate(f, 0)
            silu_gate(f, 1)
            for t in range(LC):
                inter_out(f, t)
            for t in range(LC):
                quant_down(f, t)

        @block.gpsimd
        def _(pool):
            def drives(m):
                b, j = divmod(m, STEPS)
                pool.wait_ge(act_B, m + 1)
                pool.wait_ge(du_ready, b + 1)
                if m >= RING:
                    pool.wait_ge(dve_scan, m - RING + 1)
                for h in range(HALF):
                    last = nc.gpsimd.tensor_tensor(
                        drive[:, m % RING, h], du[:, b % 2, h, :].unsqueeze(1).to_broadcast([P, NB, L]),
                        Bs[:, m % RING], ALU.mult)
                last.then_inc(pool_drive, 1)

            def fold_tile(f, t, stage):
                if stage == 0:
                    pool.wait_ge(dve_mul, LC * f + t + 1)
                    src, dst, done, gap = inter, fold, pool_stage, 4
                else:
                    pool.wait_ge(pool_stage, LC * f + t + 1)
                    src, dst, done, gap = fold, inter, pool_fold, 2
                src, dst = (v[:, t].rearrange("p (g s w) -> p g s w", s=2, w=gap * P) for v in (src, dst))
                nc.gpsimd.tensor_tensor(dst[:, :, 0, :], src[:, :, 0, :], src[:, :, 1, :], ALU.add)
                nc.gpsimd.tensor_tensor(dst[:, :, 1, :], src[:, :, 0, :], src[:, :, 1, :], ALU.subtract).then_inc(done, 1)

            def weight_scale(m):
                pool.wait_ge(dve_winv, 1)
                pool.wait_ge(ld_w[m], 16)
                nc.gpsimd.tensor_scalar(wnat[:, m], wnat[:, m], winv[:, m:m + 1], MAGIC, ALU.mult, ALU.add
                                        ).then_inc(pool_wt, 1)

            def build_hadamard():
                pool.wait_ge(ld_had, 16)
                pool.wait_ge(dve_wq, 3)
                v = had2.rearrange("p j i c -> p (j i) c")
                nc.gpsimd.tensor_copy(v[:, 0:3], had[:].unsqueeze(1).to_broadcast([P, 3, P]))
                nc.gpsimd.tensor_scalar(v[:, 3], had[:], -1.0, 1.0, ALU.mult, ALU.mult).then_inc(had_built, 1)

            nc.gpsimd.memset(dtw[:], 0.0).then_inc(zeroed, 1)
            nc.gpsimd.memset(zero_c[:], 0.0)
            nc.gpsimd.memset(one_c[:], 1.0)
            nc.gpsimd.memset(eps_c[:], LN_EPS)
            nc.gpsimd.memset(onesf[:], 1.0)
            nc.gpsimd.memset(magic_c[:], MAGIC).then_inc(consts, 1)
            for r in range(RING):
                last = nc.gpsimd.memset(decay[:, r, :, :, 0:1], 0.0)
            last.then_inc(decay_zeroed, 1)
            for m in range(AHEAD):
                drives(m)
            for k in range(B):
                p, f, n = k - 2, k - 1, k + 1
                for s in range(STEPS):
                    g = STEPS * k + s
                    if g + AHEAD < B * STEPS:
                        drives(g + AHEAD)
                    if k == 0:
                        if 2 <= s < 5:
                            weight_scale(s - 2)
                        if s == 6:
                            build_hadamard()
                    if 2 <= n < B and 1 <= s < 4:
                        if s == 1:
                            pool_front_link.begin(pool, n - 2)
                        softplus_tail(n, pool, nc.gpsimd, pool_front_link, s - 1)
                    if f >= 0:
                        if s == 6:
                            fold_tile(f, 0, 0)
                            fold_tile(f, 0, 1)
                        if s == 7:
                            fold_tile(f, 1, 0)
                    if p >= 0 and s == 0:
                        fold_tile(p, 1, 1)
            fold_tile(B - 2, 1, 1)

        @block.vector
        def _(dve):
            once = [0]

            def link_once(ins):
                once[0] += 1
                ins.then_inc(dve_once, 1)
                dve.wait_ge(dve_once, once[0])

            def newton(link, r, v, tmp):
                link(nc.vector.scalar_tensor_tensor(out=tmp, in0=r, scalar=-0.5, in1=v, op0=ALU.mult, op1=ALU.mult))
                link(nc.vector.tensor_tensor(tmp, tmp, r, ALU.mult))
                return nc.vector.scalar_tensor_tensor(out=r, in0=tmp, scalar=1.5, in1=r, op0=ALU.add, op1=ALU.mult)

            def scan(g):
                dve.wait_ge(act_decay, g + 1)
                dve.wait_ge(pool_drive, g + 1)
                if g >= STATES:
                    dve.wait_ge(dve_prod, g - STATES + 1)
                nc.vector.tensor_tensor_scan(
                    state[:, g % STATES].rearrange("p h n l -> p (h n l)"), decay[:, g % RING].rearrange("p h n l -> p (h n l)"),
                    drive[:, g % RING].rearrange("p h n l -> p (h n l)"), 0.0, ALU.mult, ALU.add).then_inc(dve_scan, 1)

            def times_C(g):
                dve.wait_ge(dve_scan, g + 1)
                dve.wait_ge(pe_C, g + 1)
                if g >= RING:
                    dve.wait_ge(pe_acc, g - RING + 1)
                nc.vector.tensor_tensor(
                    prod[:, g % RING].rearrange("p h n l -> p h (n l)"),
                    state[:, g % STATES].rearrange("p h n l -> p h (n l)"),
                    PC.unsqueeze(1).to_broadcast([P, HALF, NB * L]), ALU.mult).then_inc(dve_prod, 1)

            def norm_z(n):
                dve.wait_ge(dve_r1, 1)
                if n >= 1:
                    dve.wait_ge(act_sz, n)
                for h in range(HALF):
                    i = HALF * n + h
                    last = nc.vector.tensor_scalar(zn[:, h], xs[:, n, h], mv1[:, i, 0:1], r1[:, i:i + 1],
                                                   ALU.subtract, ALU.mult)
                last.then_inc(dve_zn, 1)

            def split(n):
                link = dve_split_link.begin(dve, n)
                k = 2 * DS
                dve.wait_ge(pe_xdbl, n + 1)
                src = front_bank(n)[0:3 * k, 0:L]
                link(nc.vector.tensor_copy(bc3[:, n], src))
                link(nc.vector.tensor_tensor(res1[:], src, bc3[:, n], ALU.subtract))
                nc.vector.tensor_copy(bc3[k:2 * k, n], res1[k:2 * k])
                link(nc.vector.tensor_copy(mid[:], res1[:]))
                nc.vector.tensor_tensor(bc3[2 * k:3 * k, n], res1[2 * k:3 * k], mid[2 * k:3 * k],
                                        ALU.subtract).then_inc(dve_split, 1)
                link.end()

            def residual(f):
                dve.wait_ge(pe_y, f + 1)
                dve.wait_ge(act_szT, f + 1)
                nc.vector.tensor_tensor(yg[:], PY[:].rearrange("p (c e) -> p c e", c=LC), szT[:],
                                        ALU.mult).then_inc(dve_x2, 1)

            def stats2(f, link):
                dve.wait_ge(dve_x2, f + 1)
                link(nc.vector.tensor_tensor(x2[:, f % 2], yg[:], xs[:, f], ALU.add))
                for c in range(LC):
                    ins = nc.vector.bn_stats(st2[:, c], x2[:, f % 2, c])
                link(ins)
                for c in range(LC):
                    ins = nc.vector.bn_aggr(mv2[:, c], st2[:, c])
                ins.then_inc(dve_stat2, 1)

            def quant_tokens(f, link):
                dve.wait_ge(dve_stat2, f + 1)
                link(nc.vector.tensor_scalar(ve2[:], mv2[:, :, 1], LN_EPS, None, ALU.add))
                dve.wait_ge(act_r2, f + 1)
                link(newton(link, r2[:], ve2[:], nt2[:]))
                for c in range(LC):
                    ins = nc.vector.tensor_scalar(xn[:, c], x2[:, f % 2, c], mv2[:, c, 0:1], r2[:, c:c + 1],
                                                  ALU.subtract, ALU.mult)
                link(ins)
                link(nc.vector.tensor_reduce(amax[:], xn[:], AX.X, ALU.max, apply_absolute_value=True))
                link(nc.vector.tensor_scalar(amax[:], amax[:], Q_EPS, 1.0 / QB, ALU.max, ALU.mult))
                link(nc.vector.reciprocal(ainv[:], amax[:]))
                for c in range(LC):
                    ins = nc.vector.tensor_scalar(xn[:, c], xn[:, c], ainv[:, c:c + 1], MAGIC, ALU.mult, ALU.add)
                link(ins)
                nc.vector.tensor_scalar(q[:], xn[:], MAGIC + QB - 1, MAGIC, ALU.min, ALU.subtract).then_inc(dve_q, 1)
                nc.vector.tensor_scalar(gs[:], amax[:], wmean[:, 0:1], None, ALU.mult)
                nc.vector.tensor_scalar(us[:], amax[:], wmean[:, 1:2], None, ALU.mult).then_inc(dve_gs, 1)
                link.end()

            def tokens_out(f):
                dve.wait_ge(pe_qT, f + 1)
                nc.vector.tensor_scalar(qT[:], X.bitcast(BF16)[:, 0:HALF * L].rearrange("p (h l) -> p h l", h=HALF),
                                        -QB, None, ALU.max).then_inc(dve_qT, 1)

            def gate_times_up(f, t):
                dve.wait_ge(act_sg, LC * f + t + 1)
                dve.wait_ge(pe_up, LC * f + t + 1)
                dve.wait_ge(dve_gs, f + 1)
                nc.vector.scalar_tensor_tensor(out=inter[:, t], in0=(GP, UP)[t][:], scalar=us[:, t:t + 1], in1=sg[:, t],
                                               op0=ALU.mult, op1=ALU.mult).then_inc(dve_mul, 1)

            def fold_last(t):
                dve.wait_ge(dve_mul, LC * (B - 1) + t + 1)
                for i in range(FOLDS):
                    src, dst = ((inter, fold), (fold, inter))[i % 2]
                    src, dst = (v[:, t].rearrange("p (g s w) -> p g s w", s=2, w=(NI >> (i + 1)) * P) for v in (src, dst))
                    nc.vector.tensor_tensor(dst[:, :, 0, :], src[:, :, 0, :], src[:, :, 1, :], ALU.add)
                    nc.vector.tensor_tensor(dst[:, :, 1, :], src[:, :, 0, :], src[:, :, 1, :], ALU.subtract
                                            ).then_inc(dve_fold, 1)
                    if i + 1 < FOLDS:
                        dve.wait_ge(dve_fold, FOLDS * t + i + 1)

            def absmax2(f, t):
                link = dve_sc_link.begin(dve, LC * f + t)
                dve.wait_ge(pe_h, LC * f + t + 1)
                a = am2[:, t:t + 1]
                link(nc.vector.tensor_reduce(a, transform_bank(f, t)[:], AX.X, ALU.max, apply_absolute_value=True))
                link(nc.vector.tensor_scalar(a, a, Q_EPS, 1.0 / QB, ALU.max, ALU.mult))
                nc.vector.reciprocal(sc2[:, t:t + 1], a).then_inc(dve_sc, 1)
                nc.vector.tensor_scalar(dq2[:, t:t + 1], a, wdn[:], None, ALU.mult).then_inc(dve_dq, 1)
                link.end()

            def round_down(f, t):
                dve.wait_ge(act_tq, LC * f + t + 1)
                nc.vector.tensor_scalar(q2[:, t], tq, MAGIC + QB - 1, MAGIC, ALU.min, ALU.subtract).then_inc(dve_q2, 1)

            def q2_out(f, t):
                dve.wait_ge(pe_q2T, LC * f + t + 1)
                nc.vector.tensor_scalar(q2T[:, t], q2_bank(f, t).bitcast(BF16).rearrange("p (a c) -> p a c", a=NI),
                                        -QB, None, ALU.max).then_inc(dve_q2T, 1)

            def result(f, t):
                dve.wait_ge(pe_dn, LC * f + t + 1)
                dve.wait_ge(dve_dq, LC * f + t + 1)
                if f >= 1:
                    dve.wait_ge(stored[t], 16 * f)
                nc.vector.scalar_tensor_tensor(out=ot[:, t], in0=down_bank(f, t)[:, 0:E], scalar=dq2[:, t:t + 1],
                                               in1=x2[:, f % 2, t], op0=ALU.mult, op1=ALU.add).then_inc(dve_out, 1)

            def weight_abs(m):
                dve.wait_ge(ld_w[m], 16)
                nc.vector.tensor_reduce(wsum[:, m:m + 1], wnat[:, m], AX.X, ALU.add,
                                        apply_absolute_value=True).then_inc(wabs_done, 1)

            def weight_means():
                dve.wait_ge(pe_wsum, 1)
                dve.wait_ge(act_gate, 1)
                link_once(nc.vector.tensor_scalar(wmean[:], bank7[:, 0:3], 1.0 / (2 * P * I), Q_EPS, ALU.mult, ALU.max))
                nc.vector.tensor_tensor(wdn[:], wmean[:, 2:3], tg[:, 1:2], ALU.mult)
                nc.vector.reciprocal(winv[:], wmean[:]).then_inc(dve_winv, 1)

            def weight_round(m):
                dve.wait_ge(pool_wt, m + 1)
                nc.vector.tensor_scalar(wq[:, m], wnat[:, m], MAGIC + 1.0, MAGIC, ALU.min, ALU.subtract).then_inc(dve_wq, 1)

            def weight_out(i):
                dve.wait_ge(pe_wT, i + 1)
                nc.vector.tensor_scalar(wT[:].rearrange("p m n -> p (m n)")[:, I * i:I * (i + 1)],
                                        (bank7 if i % 2 == 0 else bank6).bitcast(BF16), -1.0, None, ALU.max
                                        ).then_inc(dve_wT, 1)

            def first_norm():
                dve.wait_ge(ld_x, 16)
                for i in range(B * LC):
                    last = nc.vector.bn_stats(st1[:, i], xs[:, i // LC, i % LC])
                link_once(last)
                for i in range(B * LC):
                    last = nc.vector.bn_aggr(mv1[:, i], st1[:, i])
                last.then_inc(dve_stat1, 1)
                dve.wait_ge(dve_stat1, 1)
                link_once(nc.vector.tensor_scalar(ve1[:], mv1[:, :, 1], LN_EPS, None, ALU.add))

            dve.wait_ge(ld_consts, 16)
            nc.vector.tensor_copy(id16[:], id32[:])
            for i in range(3):
                k = slice(2 * DS * i, 2 * DS * (i + 1))
                last = nc.vector.tensor_copy(sel[k, :], id32[k, k])
            last.then_inc(dve_consts, 1)
            dve.wait_ge(ld_inw, 16)
            dve.wait_ge(ld_taps, 16)
            for k in range(DC):
                for h in range(HALF):
                    last = nc.vector.tensor_scalar(inwk[:, k, h], inw[:, h], cw[:, h, k:k + 1], None, ALU.mult)
                if k % 2 == 1:
                    last.then_inc(dve_inwk, 1)
            first_norm()
            split(0)
            dve.wait_ge(act_gate, 2)
            nc.vector.tensor_scalar(aneg[:], aneg[:], -1.0, None, ALU.mult).then_inc(dve_aneg, 1)
            weight_abs(1)
            dve_front_link.begin(dve, 0)
            for part in range(3):
                softplus_tail(0, dve, nc.vector, dve_front_link, part)
            scan(0)
            for k in range(B):
                p, f, n = k - 2, k - 1, k + 2
                old, new, front = p >= 0, f >= 0, n < B
                for s in range(STEPS):
                    g = STEPS * k + s
                    if k == 0 and s == 0:
                        dve.wait_ge(act_r1, 2)
                        newton(link_once, r1[:], ve1[:], nt1[:]).then_inc(dve_r1, 1)
                        norm_z(0)
                    if g + 1 < B * STEPS:
                        scan(g + 1)
                    if s == 0 and new:
                        residual(f)
                    if s == 6 and new:
                        gate_times_up(f, 1)
                    if old:
                        if s == 1:
                            absmax2(p, 0)
                        if s == 2:
                            round_down(p, 0)
                        if s == 3:
                            absmax2(p, 1)
                        if s == 4:
                            round_down(p, 1)
                    times_C(g)
                    if s == 0:
                        if new:
                            stats2(f, dve_ln_link.begin(dve, f))
                        if k == 0:
                            weight_abs(2)
                    if s == 1:
                        if new:
                            quant_tokens(f, dve_ln_link)
                        if k == 0:
                            split(1)
                    if s == 2:
                        if new:
                            tokens_out(f)
                        if old:
                            q2_out(p, 0)
                        if k == 0:
                            weight_means()
                    if s == 3:
                        if old:
                            result(p, 0)
                        if k == 0:
                            dve_front_link.begin(dve, 1)
                            for part in range(3):
                                softplus_tail(1, dve, nc.vector, dve_front_link, part)
                        if k + 1 < B:
                            norm_z(k + 1)
                    if s == 4 and old:
                        q2_out(p, 1)
                    if s == 5:
                        if new:
                            gate_times_up(f, 0)
                        if old:
                            result(p, 1)
                    if s == 6 and front:
                        split(n)
                    if k == 0 and s >= 4:
                        for m in ((0, 1), (2,), (), ())[s - 4]:
                            weight_round(m)
                        for i in ((), (0, 1), (2, 3), (4, 5))[s - 4]:
                            weight_out(i)
            p, f = B - 2, B - 1
            residual(f)
            stats2(f, dve_ln_link.begin(dve, f))
            absmax2(p, 0)
            quant_tokens(f, dve_ln_link)
            round_down(p, 0)
            tokens_out(f)
            absmax2(p, 1)
            q2_out(p, 0)
            round_down(p, 1)
            gate_times_up(f, 0)
            result(p, 0)
            fold_last(0)
            q2_out(p, 1)
            gate_times_up(f, 1)
            fold_last(1)
            result(p, 1)
            absmax2(f, 0)
            round_down(f, 0)
            q2_out(f, 0)
            absmax2(f, 1)
            result(f, 0)
            round_down(f, 1)
            q2_out(f, 1)
            result(f, 1)


def tiles(t):
    return t.rearrange("b l n -> (b l) n").rearrange("(c p) n -> p c n", p=P)


_INS = ['x', 'ctx_1024', 'g_xattn', 'g_ffn', 'L0_xattn_in_proj_w', 'L0_xattn_conv_w', 'L0_xattn_conv_b',
        'L0_xattn_x_proj_w', 'L0_xattn_dt_proj_w', 'L0_xattn_dt_proj_b', 'L0_xattn_A_log', 'L0_xattn_D',
        'L0_ffn_w_gate', 'L0_ffn_w_up', 'L0_ffn_w_down']


def _constants():
    import numpy as np
    h = np.ones((1, 1), np.float32)
    while h.shape[0] < P:
        h = np.block([[h, h], [h, -h]])
    return {"ident": np.eye(P, dtype=np.float32), "hadamard": (h / math.sqrt(I)).astype(np.float32)}


def kernel(**inputs):
    import numpy as np
    import concourse.bacc as bacc
    from concourse.bass_utils import run_bass_kernel_spmd

    nc = bacc.Bacc("TRN2", target_bir_lowering=False, num_devices=1)
    arrays, args = {}, []
    for name, a in [(n, np.ascontiguousarray(inputs[n])) for n in _INS] + list(_constants().items()):
        arrays[f"in_{name}_dram"] = a
        args.append(nc.dram_tensor(f"in_{name}_dram", a.shape, mybir.dt.from_np(a.dtype), kind="ExternalInput").ap())
    out = nc.dram_tensor("out_0_dram", (B, L, E), F32, kind="ExternalOutput").ap()
    gated_ssm_ffn(nc, *args, out)
    return run_bass_kernel_spmd(nc, [arrays], core_ids=[0]).results[0]["out_0_dram"]
```

```python
import math
from contextlib import ExitStack

import concourse.bass as bass
from concourse import mybir

F32 = mybir.dt.float32
BF16 = mybir.dt.bfloat16
ALU = mybir.AluOpType
ACT = mybir.ActivationFunctionType
AX = mybir.AxisListType

P = 128
B, L, E = 4, 256, 256
DM, DS, DR, DC = 128, 16, 8, 4
I = 1024
HALF = E // P
LC = L // P
NI = I // P
NB = 2
STEPS = DS // NB
DVE_DRIVES = 2
AHEAD = 4
RING = 4
STATES = 3
LN_EPS = 1e-5
Q_EPS = 1e-5
QB = 128.0
MAGIC = 1.5 * 2.0 ** 23
FOLDS = NI.bit_length() - 1
DVE_COLS = 88
DT0 = 96


class Chain:

    def __init__(self, sem, per_batch):
        self.sem, self.per_batch = sem, per_batch

    def begin(self, eng, batch):
        self.eng, self.base, self.count = eng, batch * self.per_batch, 0
        return self

    def __call__(self, ins):
        self.count += 1
        ins.then_inc(self.sem, 1)
        self.eng.wait_ge(self.sem, self.base + self.count)

    def end(self):
        assert self.count == self.per_batch, (self.count, self.per_batch)


def gated_ssm_ffn(nc, x, ctx_1024, g_xattn, g_ffn, in_proj_w, conv_w, conv_b, x_proj_w, dt_proj_w, dt_proj_b,
                  A_log, D, w_gate, w_up, w_down, ident, hadamard, out):
    stack = ExitStack()
    with stack:
        def sb(name, shape, dt=F32):
            return stack.enter_context(nc.sbuf_tensor(name, shape, dt))

        def sem(name):
            return stack.enter_context(nc.semaphore(name))

        xs = sb("xs", [P, B, LC, E])
        ctxs = sb("ctxs", [P, B, LC, DM])
        ctxT = sb("ctxT", [DM, B, L])
        id32 = sb("id32", [P, P])
        id16 = sb("id16", [P, P], BF16)
        had = sb("had", [P, P])
        sel = sb("sel", [3 * 2 * DS, 2 * DS], BF16)
        inw = sb("inw", [P, HALF, DM])
        inwk = sb("inwk", [P, DC, HALF, DM])
        inwT = sb("inwT", [DM, DC, E])
        xpw = sb("xpw", [DR + 2 * DS, E])
        xpwT = sb("xpwT", [P, HALF, DT0 + DR])
        dtw = sb("dtw", [P, HALF, DT0 + DR])
        dtwT = sb("dtwT", [DT0 + DR, E])
        cw = sb("cw", [P, HALF, DC])
        cb = sb("cb", [P, HALF])
        dtb = sb("dtb", [P, HALF])
        dskip = sb("dskip", [P, HALF])
        alog = sb("alog", [P, HALF, DS])
        aneg = sb("aneg", [P, HALF, DS])
        gates = sb("gates", [P, 2])
        tg = sb("tg", [P, 2])
        onesf = sb("onesf", [P, P])
        eps_c = sb("eps_c", [P, 1])
        one_c = sb("one_c", [P, 1])
        magic_c = sb("magic_c", [P, 1])
        zero_c = sb("zero_c", [P, 1])
        st1 = sb("st1", [P, B * LC, 6])
        mv1 = sb("mv1", [P, B * LC, 2])
        ln1 = sb("ln1", [P, B * LC])
        r1 = sb("r1", [P, B * LC])
        nt1 = sb("nt1", [P, B * LC])
        mr1 = sb("mr1", [P, B * LC])
        ve1 = sb("ve1", [P, B * LC])
        zn = sb("zn", [P, HALF, L])
        sz = sb("sz", [P, HALF, L])
        szT = sb("szT", [P, LC, E])
        conv = sb("conv", [P, HALF, L])
        u = sb("u", [P, 3, HALF, L])
        bc3 = sb("bc3", [3 * 2 * DS, B, L], BF16)
        high = sb("high", [2 * 2 * DS, L], BF16)
        rest = sb("rest", [2 * 2 * DS, L])
        dtlo = sb("dtlo", [DT0 + DR, L])
        spa = sb("spa", [P, HALF, L])
        spe = sb("spe", [P, HALF, L])
        spl = sb("spl", [P, HALF, L])
        spr = sb("spr", [P, HALF, L])
        spm = spa
        delta = sb("delta", [P, 2, HALF, L])
        du = sb("du", [P, 2, HALF, L])
        diag = sb("diag", [P, HALF, P])
        Bs = sb("Bs", [P, RING, NB, L])
        decay = sb("decay", [P, RING, HALF, NB, L])
        drive = sb("drive", [P, RING, HALF, NB, L])
        state = sb("state", [P, STATES, HALF, NB, L])
        prod = sb("prod", [P, RING, HALF, NB, L])
        x2 = sb("x2", [P, 2, LC, E])
        st2 = sb("st2", [P, LC, 6])
        mv2 = sb("mv2", [P, LC, 2])
        ve2 = sb("ve2", [P, LC])
        ln2 = sb("ln2", [P, LC])
        r2 = sb("r2", [P, LC])
        nt2 = sb("nt2", [P, LC])
        mr2 = sb("mr2", [P, LC])
        xn = sb("xn", [P, LC, E])
        yg = xn
        inw0T = xn[:, 0]
        amax = sb("amax", [P, LC])
        ainv = sb("ainv", [P, LC])
        gs = sb("gs", [P, LC])
        us = sb("us", [P, LC])
        q = sb("q", [P, LC, E], BF16)
        qT = sb("qT", [P, HALF, L], BF16)
        wnat = sb("wnat", [P, 3, 2 * I])
        wq = sb("wq", [P, 3, 2 * I], BF16)
        wT = sb("wT", [P, 3, 2 * I], BF16)
        hT = sb("hT", [P, LC, NI, P])
        wsum = sb("wsum", [P, 3])
        wmean = sb("wmean", [P, 3])
        winv = sb("winv", [P, 3])
        wdn = sb("wdn", [P, 1])
        inter = wnat[:, 0].rearrange("p (t n) -> p t n", t=LC)
        had2 = wnat[:, 2, 0:4 * P].rearrange("p (j i c) -> p j i c", j=2, i=2)
        fold = wnat[:, 1].rearrange("p (t n) -> p t n", t=LC)
        sg = wq[:, 0:2].rearrange("p m n -> p (m n)").bitcast(F32).rearrange("p (t n) -> p t n", t=LC)
        am2 = sb("am2", [P, LC])
        sc2 = sb("sc2", [P, LC])
        dq2 = sb("dq2", [P, LC])
        tq = ctxs[:].rearrange("p b c d -> p (b c d)")
        q2 = wq[:, 2].rearrange("p (t n) -> p t n", t=LC)
        q2T = sb("q2T", [P, LC, NI, P], BF16)
        ot = sb("ot", [P, LC, E])

        BC, GP, UP = (stack.enter_context(nc.psum_tensor(n, [P, 2 * 512], F32)) for n in ("BC", "GP", "UP"))
        PB, PC = BC[:, 0:512], BC[:, 512:1024]
        PY = stack.enter_context(nc.psum_tensor("PY", [P, 512], F32))
        X = stack.enter_context(nc.psum_tensor("X", [P, 512], F32))[:]
        bank4, bank5 = GP[:, 0:512], GP[:, 512:1024]
        bank6, bank7 = UP[:, 0:512], UP[:, 512:1024]

        wgT = wT[:, 0].rearrange("p (h i) -> p h i", h=HALF)
        wuT = wT[:, 1].rearrange("p (h i) -> p h i", h=HALF)
        wdT = wT[:, 2].rearrange("p (a o) -> p a o", a=NI)

        ld_consts, ld_ctx0, ld_inw, ld_taps, ld_small, ld_ctx, ld_x, ld_had, ld_gate = (
            sem(n) for n in ("ld_consts", "ld_ctx0", "ld_inw", "ld_taps", "ld_small", "ld_ctx", "ld_x", "ld_had",
                             "ld_gate"))
        ld_conv, ld_w = sem("ld_conv"), [sem(f"ld_w{i}") for i in range(3)]
        zeroed, consts, decay_zeroed = sem("zeroed"), sem("consts"), sem("decay_zeroed")
        pe_setup, act_setup, dve_setup = sem("pe_setup"), sem("act_setup"), sem("dve_setup")
        act_gate, dve_aneg, dve_consts = sem("act_gate"), sem("dve_aneg"), sem("dve_consts")
        dve_stat1, act_r1, dve_r1 = sem("dve_stat1"), sem("act_r1"), sem("dve_r1")
        wabs_done, pe_wsum, dve_winv, pool_wt, dve_wq, pe_wT, dve_wT = (
            sem(n) for n in ("wabs_done", "pe_wsum", "dve_winv", "pool_wt", "dve_wq", "pe_wT", "dve_wT"))
        act_tap, dve_conv, dve_drive = sem("act_tap"), sem("dve_conv"), sem("dve_drive")
        had_built, dve_fold, pool_fold_last = sem("had_built"), sem("dve_fold"), sem("pool_fold_last")
        pe_B, act_B, act_decay, pool_drive, dve_scan, pe_C, dve_prod, pe_acc = (
            sem(n) for n in ("pe_B", "act_B", "act_decay", "pool_drive", "dve_scan", "pe_C", "dve_prod", "pe_acc"))
        pe_xin, dve_inwk, act_conv, act_u, pe_xdbl, dve_split, act_dtlo, pe_draw = (
            sem(n) for n in ("pe_xin", "dve_inwk", "act_conv", "act_u", "pe_xdbl", "dve_split", "act_dtlo", "pe_draw"))
        act_spread, act_sp, delta_ready, du_ready, pool_zn, act_sz, pe_szT, act_szT, pe_y, dve_x2 = (
            sem(n) for n in ("act_spread", "act_sp", "delta_ready", "du_ready", "pool_zn", "act_sz", "pe_szT", "act_szT",
                             "pe_y", "dve_x2"))
        act_high, act_high0, pool_diag = sem("act_high"), sem("act_high0"), sem("pool_diag")
        dve_r2, act_xn, dve_ainv, act_xr = (sem(n) for n in ("dve_r2", "act_xn", "dve_ainv", "act_xr"))
        dve_stat2, act_r2, dve_q, pe_qT, dve_qT, pe_gate, pe_up, act_sg, dve_mul = (
            sem(n) for n in ("dve_stat2", "act_r2", "dve_q", "pe_qT", "dve_qT", "pe_gate", "pe_up", "act_sg", "dve_mul"))
        pool_fold, pe_tp, act_tp, pe_h, dve_sc, act_tq, dve_q2, pe_q2T, dve_q2T, pe_dn, dve_out = (
            sem(n) for n in ("pool_fold", "pe_tp", "act_tp", "pe_h", "dve_sc", "act_tq", "dve_q2", "pe_q2T", "dve_q2T",
                             "pe_dn", "dve_out"))
        stored = [sem(f"stored_{t}") for t in range(LC)]
        pool_front_link = Chain(sem("pool_front_link"), 4)
        dve_front_link = Chain(sem("dve_front_link"), 3)
        dve_once = sem("dve_once")
        act_r2_link = Chain(sem("act_r2_link"), 1)
        act_sp_link = Chain(sem("act_sp_link"), 1)
        pool_stage = sem("pool_stage")
        dve_split_link = Chain(sem("dve_split_link"), 1)
        dve_gs, dve_dq = sem("dve_gs"), sem("dve_dq")
        dve_ln_link = Chain(sem("dve_ln_link"), 8)
        dve_sc_link = Chain(sem("dve_sc_link"), 2)

        block = stack.enter_context(nc.Block())

        def front_bank(n):
            return bank4 if n < 2 else X

        def dt_bank(n):
            return bank5 if n == 0 else front_bank(n)

        def transform_bank(f, t):
            return BC if (f, t) in ((B - 2, 1), (B - 1, 0)) else UP

        def q2_bank(f, t):
            return (bank4 if t == 0 else X) if f < B - 2 else (X if (f, t) == (B - 1, 1) else PY[:])

        def down_bank(f, t):
            return bank5 if f < B - 2 and t == 0 else q2_bank(f, t)

        def drives_before(m):
            return m - DVE_DRIVES

        def du_of(n, eng, ops):
            if n >= 2:
                eng.wait_ge(pool_drive, drives_before(STEPS * (n - 1)))
            eng.wait_ge(delta_ready, n + 1)
            ops.tensor_tensor(du[:, n % 2], delta[:, n % 2], u[:, n % 3], ALU.mult).then_inc(du_ready, 1)

        def softplus_tail(n, eng, ops, link, part):
            if part == 0:
                eng.wait_ge(act_sp, n + 1)
                link(ops.tensor_scalar(spm[:], spe[:], 1.0, 1.0, ALU.mult, ALU.add))
                link(ops.tensor_scalar(spm[:], spm[:], 1.0, -1.0, ALU.mult, ALU.add))
                link(ops.tensor_tensor(spm[:], spm[:], spe[:], ALU.subtract))
            if part == 1:
                eng.wait_ge(act_decay, STEPS * (n - 1))
                link(ops.tensor_tensor(spl[:], spl[:], spm[:], ALU.subtract))
                ops.tensor_tensor(delta[:, n % 2], spl[:], spr[:], ALU.add).then_inc(delta_ready, 1)
            if part == 2:
                du_of(n, eng, ops)
                link.end()

        def fold_last(t, eng, ops, cols, done):
            eng.wait_ge(dve_mul, LC * (B - 1) + t + 1)
            for i in range(FOLDS):
                src, dst = ((inter, fold), (fold, inter))[i % 2]
                src, dst = (v[:, t].rearrange("p (g s w c) -> p g s w c", s=2, w=NI >> (i + 1), c=P)[:, :, :, :, cols]
                            for v in (src, dst))
                ops.tensor_tensor(dst[:, :, 0], src[:, :, 0], src[:, :, 1], ALU.add)
                ops.tensor_tensor(dst[:, :, 1], src[:, :, 0], src[:, :, 1], ALU.subtract).then_inc(done, 1)
                if i + 1 < FOLDS:
                    eng.wait_ge(done, FOLDS * t + i + 1)

        @block.sync
        def _(sp):
            cr = tiles(ctx_1024)
            sp.dma_start(ctxs[:, 0], cr[:, 0:LC]).then_inc(ld_ctx0, 16)
            sp.dma_start(inw[:], in_proj_w.rearrange("(h p) d -> p h d", p=P)).then_inc(ld_inw, 16)
            sp.dma_start(xpw[:], x_proj_w).then_inc(ld_small, 16)
            sp.wait_ge(zeroed, 1)
            sp.dma_start(dtw[:, :, DT0:DT0 + DR], dt_proj_w.rearrange("(h p) r -> p h r", p=P)).then_inc(ld_small, 16)
            with nc.allow_non_contiguous_dma(reason="one value per partition"):
                for dst, src in ((cb, conv_b), (dtb, dt_proj_b), (dskip, D)):
                    sp.dma_start(dst[:], src.rearrange("(h p) -> p h", p=P)).then_inc(ld_conv, 16)
            sp.dma_start(ctxs[:, 1:B].rearrange("p b c d -> p (b c) d"), cr[:, LC:B * LC]).then_inc(ld_ctx, 16)
            sp.dma_start(wnat[:, 0].rearrange("p (a h) -> p a h", a=NI),
                         w_gate.rearrange("(a p) h -> p a h", p=P)).then_inc(ld_w[0], 16)
            sp.dma_start(xs[:].rearrange("p b c d -> p (b c) d"), tiles(x)).then_inc(ld_x, 16)
            sp.dma_start(wnat[:, 1].rearrange("p (a h) -> p a h", a=NI),
                         w_up.rearrange("(a p) h -> p a h", p=P)).then_inc(ld_w[1], 16)
            sp.dma_start(wnat[:, 2].rearrange("p (o i) -> p o i", o=HALF),
                         w_down.rearrange("(o p) i -> p o i", p=P)).then_inc(ld_w[2], 16)
            sp.dma_start(had[:], hadamard).then_inc(ld_had, 16)
            for b in range(B):
                for t in range(LC):
                    sp.wait_ge(dve_out, LC * b + t + 1)
                    sp.dma_start(tiles(out)[:, LC * b + t], ot[:, t]).then_inc(stored[t], 16)
            for t in range(LC):
                sp.wait_ge(stored[t], 16 * B)

        @block.tensor
        def _(pe):
            def setup():
                pe.wait_ge(ld_consts, 16)
                pe.wait_ge(ld_ctx0, 16)
                for c in range(LC):
                    last = nc.tensor.transpose(bank4[:, P * c:P * (c + 1)], ctxs[:, 0, c], id32[:])
                last.then_inc(pe_setup, 1)
                pe.wait_ge(ld_inw, 16)
                for h in range(HALF):
                    last = nc.tensor.transpose(bank5[:, P * h:P * (h + 1)], inw[:, h], id32[:])
                last.then_inc(pe_setup, 1)

            def setup_weights():
                pe.wait_ge(ld_small, 16 * 2)
                for h in range(HALF):
                    last = nc.tensor.transpose(PY[:, P * h:P * h + DR + 2 * DS], xpw[:, P * h:P * (h + 1)],
                                               id32[0:DR + 2 * DS, 0:DR + 2 * DS])
                last.then_inc(pe_setup, 1)
                for h in range(HALF):
                    last = nc.tensor.transpose(PB[0:DT0 + DR, P * h:P * (h + 1)], dtw[:, h], id32[:])
                last.then_inc(pe_setup, 1)
                pe.wait_ge(dve_inwk, 2)
                for k in range(DC):
                    for h in range(HALF):
                        last = nc.tensor.transpose(UP[:, E * k + P * h:E * k + P * (h + 1)], inwk[:, k, h], id32[:])
                last.then_inc(pe_setup, 1)

            def first_in_proj():
                pe.wait_ge(dve_setup, 2)
                for h in range(HALF):
                    last = nc.tensor.matmul(bank4[:, L * h:L * (h + 1)], inw0T[:, P * h:P * (h + 1)], ctxT[:, 0, :],
                                            start=True, stop=True)
                last.then_inc(pe_xin, 1)

            def setup_late():
                pe.wait_ge(ld_ctx, 16)
                pe.wait_ge(act_setup, 1)
                for b in range(1, B):
                    for c in range(LC):
                        at = (b - 1) * L + P * c
                        last = nc.tensor.transpose((PC if at < 512 else PY)[:, at % 512:at % 512 + P], ctxs[:, b, c], id32[:])
                last.then_inc(pe_setup, 1)

            def B_rows(m):
                b, j = divmod(m, STEPS)
                pe.wait_ge(dve_split, b + 1)
                pe.wait_ge(act_high0, b + 1)
                if m >= 1:
                    pe.wait_ge(act_B, m)
                else:
                    pe.wait_ge(act_setup, 2)
                for n in range(NB):
                    last = nc.tensor.matmul(PB[:, L * n:L * (n + 1)], row_pick(NB * j + n), bc3[:, b, :],
                                            start=True, stop=True)
                last.then_inc(pe_B, 1)

            def C_rows(m):
                b, j = divmod(m, STEPS)
                pe.wait_ge(dve_split, b + 1)
                pe.wait_ge(act_high0, b + 1)
                if m >= 1:
                    pe.wait_ge(dve_prod, m)
                else:
                    pe.wait_ge(act_setup, 4)
                for n in range(NB):
                    last = nc.tensor.matmul(PC[:, L * n:L * (n + 1)], row_pick(DS + NB * j + n), bc3[:, b, :],
                                            start=True, stop=True)
                last.then_inc(pe_C, 1)

            def row_pick(r):
                return sel[:, r:r + 1].to_broadcast([3 * 2 * DS, P])

            def accumulate(g):
                b, j = divmod(g, STEPS)
                pe.wait_ge(dve_prod, g + 1)
                if j == 0 and b >= 1:
                    pe.wait_ge(dve_x2, b)
                for h in range(HALF):
                    for n in range(NB):
                        for c in range(LC):
                            last = nc.tensor.matmul(PY[:, E * c + P * h:E * c + P * (h + 1)],
                                                    prod[:, g % RING, h, n, P * c:P * (c + 1)], id32[:],
                                                    is_transpose=True, start=(j == 0 and h == n == c == 0), stop=False,
                                                    skip_group_check=True)
                last.then_inc(pe_acc, 1)
                if j == STEPS - 1:
                    pe.wait_ge(pool_diag, 1)
                    for h in range(HALF):
                        for c in range(LC):
                            last = nc.tensor.matmul(PY[:, E * c + P * h:E * c + P * (h + 1)],
                                                    u[:, b % 3, h, P * c:P * (c + 1)], diag[:, h],
                                                    start=False, stop=(h == HALF - 1 and c == LC - 1),
                                                    skip_group_check=True)
                    last.then_inc(pe_y, 1)

            def in_proj(n, halves=range(HALF)):
                if n == 1:
                    pe.wait_ge(act_setup, 4)
                    pe.wait_ge(dve_split, n)
                    pe.wait_ge(act_high0, n)
                    pe.wait_ge(act_dtlo, n)
                elif n == 2:
                    pass
                else:
                    pe.wait_ge(dve_qT, n - 2)
                for h in halves:
                    for d in range(DC):
                        last = nc.tensor.matmul(front_bank(n)[:, L * h + d:L * (h + 1)],
                                                inwT[:, DC - 1 - d, P * h:P * (h + 1)], ctxT[:, n, 0:L - d],
                                                start=(d == 0), stop=(d == DC - 1))
                if h == HALF - 1:
                    last.then_inc(pe_xin, 1)

            def x_dbl(n):
                pe.wait_ge(act_u, n + 1)
                if n == 0:
                    pe.wait_ge(act_setup, 1)
                if n >= 2:
                    pe.wait_ge(act_conv, n - 1)
                if n >= 4:
                    pe.wait_ge(dve_out, LC * (n - 3))
                for h in range(HALF):
                    last = nc.tensor.matmul(front_bank(n)[0:DT0 + DR, 0:L], xpwT[:, h, :], u[:, n % 3, h, :],
                                            start=(h == 0), stop=(h == HALF - 1))
                last.then_inc(pe_xdbl, 1)

            def dt_proj(n):
                pe.wait_ge(act_dtlo, n + 1)
                if n == 0:
                    pe.wait_ge(act_setup, 2)
                else:
                    pe.wait_ge(dve_split, n + 1)
                    pe.wait_ge(act_high0, n + 1)
                for h in range(HALF):
                    last = nc.tensor.matmul(dt_bank(n)[:, L * h:L * (h + 1)], dtwT[DT0:DT0 + DR, P * h:P * (h + 1)],
                                            dtlo[DT0:DT0 + DR, :], start=True, stop=True)
                last.then_inc(pe_draw, 1)

            def gate_T(k):
                pe.wait_ge(act_sz, k + 1)
                if k >= 1 and k + 1 < B:
                    pe.wait_ge(act_spread, k + 2)
                if k + 1 == B:
                    pe.wait_ge(dve_out, LC * (k - 2))
                for h in range(HALF):
                    for c in range(LC):
                        last = nc.tensor.transpose((bank5 if k == 0 else X)[:, E * c + P * h:E * c + P * (h + 1)],
                                                   sz[:, h, P * c:P * (c + 1)], id32[:])
                last.then_inc(pe_szT, 1)

            def tokens_T(f):
                pe.wait_ge(dve_q, f + 1)
                if f + 1 < B:
                    pe.wait_ge(act_szT, f + 2)
                else:
                    pe.wait_ge(dve_out, LC * (f - 1))
                for c in range(LC):
                    for h in range(HALF):
                        last = nc.tensor.transpose(X.bitcast(BF16)[:, L * h + P * c:L * h + P * (c + 1)],
                                                   q[:, c, P * h:P * (h + 1)], id16[:])
                last.then_inc(pe_qT, 1)

            def gate(f, t):
                pe.wait_ge(dve_qT, f + 1)
                if f == 0 and t == 0:
                    pe.wait_ge(dve_wT, 6)
                    pe.wait_ge(act_spread, 2)
                    pe.wait_ge(act_szT, 1)
                elif t == 0 and f < B - 1:
                    pe.wait_ge(dve_out, LC * (f - 1) + 1)
                elif t == 0:
                    pe.wait_ge(act_tp, LC * f)
                elif 0 < f < B - 1:
                    pe.wait_ge(act_tq, LC * f)
                elif f == B - 1:
                    pe.wait_ge(act_tq, LC * f - 1)
                tokens_by(f, t, wgT, pe_gate)

            def up(f, t):
                pe.wait_ge(act_sg, LC * f + t + 1)
                tokens_by(f, t, wuT, pe_up)

            def tokens_by(f, t, w, done):
                for i in range(2):
                    for h in range(HALF):
                        last = nc.tensor.matmul((GP, UP)[t][:, 512 * i:512 * (i + 1)], qT[:, h, P * t:P * (t + 1)],
                                                w[:, h, 512 * i:512 * (i + 1)],
                                                start=(h == 0), stop=(h == HALF - 1))
                last.then_inc(done, 1)

            def inter_T(f, t):
                if f < B - 1:
                    pe.wait_ge(pool_fold, LC * f + t + 1)
                else:
                    pe.wait_ge(dve_fold, FOLDS * (t + 1))
                    pe.wait_ge(pool_fold_last, FOLDS * (t + 1))
                if t == 1:
                    pe.wait_ge(act_tp, LC * f + 1)
                src = inter if f < B - 1 else fold
                for a in range(NI):
                    last = nc.tensor.transpose(GP[:, P * a:P * (a + 1)], src[:, t, P * a:P * (a + 1)], id32[:])
                last.then_inc(pe_tp, 1)

            def hadamard_mm(f, t):
                pe.wait_ge(act_tp, LC * f + t + 1)
                if f == t == 0:
                    pe.wait_ge(had_built, 1)
                if (f, t) == (B - 2, 1):
                    pe.wait_ge(act_B, B * STEPS)
                    pe.wait_ge(dve_prod, B * STEPS)
                elif (f, t) == (B - 1, 0):
                    pe.wait_ge(act_tq, LC * f)
                elif f == B - 1:
                    pe.wait_ge(dve_mul, LC * f + 2)
                elif t == 0:
                    pe.wait_ge(dve_mul, LC * f + 2)
                else:
                    pe.wait_ge(act_tq, LC * f + 1)
                dst = transform_bank(f, t)
                for a in range(NI):
                    if f < B - 1:
                        last = nc.tensor.matmul(dst[:, E * (a // 2):E * (a // 2 + 1)], hT[:, t, a, :],
                                                had2[:, a % 2].rearrange("p i c -> p (i c)"),
                                                start=(a % 2 == 0), stop=(a % 2 == 1))
                    else:
                        last = nc.tensor.matmul(dst[:, P * a:P * (a + 1)], hT[:, t, a, :], had2[:, 0, 0],
                                                start=True, stop=True)
                last.then_inc(pe_h, 1)

            def q2_T(f, t):
                pe.wait_ge(dve_q2, LC * f + t + 1)
                if f < B - 2 and t == 0:
                    pe.wait_ge(act_tp, LC * f + 2)
                elif f < B - 2:
                    pe.wait_ge(dve_qT, f + 2)
                    if f + 4 < B:
                        pe.wait_ge(act_conv, f + 3)
                elif (f, t) == (B - 2, 0):
                    pe.wait_ge(dve_x2, B)
                elif (f, t) != (B - 1, 1):
                    pe.wait_ge(dve_out, LC * f + t)
                else:
                    pe.wait_ge(dve_qT, B)
                for a in range(NI):
                    last = nc.tensor.transpose(q2_bank(f, t).bitcast(BF16)[:, P * a:P * (a + 1)],
                                               q2[:, t, P * a:P * (a + 1)], id16[:])
                last.then_inc(pe_q2T, 1)

            def down(f, t):
                pe.wait_ge(dve_q2T, LC * f + t + 1)
                for a in range(NI):
                    last = nc.tensor.matmul(down_bank(f, t)[:, 0:E], q2T[:, t, a, :], wdT[:, a, :],
                                            start=(a == 0), stop=(a == NI - 1))
                last.then_inc(pe_dn, 1)

            def weight_sum():
                pe.wait_ge(wabs_done, 3)
                pe.wait_ge(act_setup, 3)
                nc.tensor.matmul(bank7[:, 0:3], onesf[:], wsum[:], start=True, stop=True).then_inc(pe_wsum, 1)

            def weight_T(i):
                m, part = divmod(i, 2)
                pe.wait_ge(dve_wq, m + 1)
                if i == 0:
                    pe.wait_ge(dve_winv, 1)
                if i >= 2:
                    pe.wait_ge(dve_wT, i - 1)
                bk = (bank7 if i % 2 == 0 else bank6).bitcast(BF16)
                for k in range(8):
                    if m < 2:
                        blk = wq[:, m].rearrange("p (a h c) -> p h a c", a=NI, h=HALF)[:, part, k, :]
                    else:
                        a, oh = 4 * part + k // 2, k % 2
                        blk = wq[:, m].rearrange("p (o a c) -> p o a c", o=HALF, a=NI)[:, oh, a, :]
                    last = nc.tensor.transpose(bk[:, P * k:P * (k + 1)], blk, id16[:])
                last.then_inc(pe_wT, 1)

            setup()
            first_in_proj()
            setup_weights()
            pe.wait_ge(dve_consts, 1)
            x_dbl(0)
            dt_proj(0)
            B_rows(0)
            setup_late()
            B_rows(1)
            in_proj(1, [0])
            B_rows(2)
            in_proj(1, [1])
            C_rows(0)
            for m in range(3, AHEAD):
                B_rows(m)
            for k in range(B):
                p, f, n = k - 2, k - 1, k + 2
                old, new, front = p >= 0, f >= 0, n < B
                for s in range(STEPS):
                    g = STEPS * k + s
                    if s == 2:
                        if old:
                            inter_T(p, 1)
                        if k == 0:
                            weight_sum()
                    if s == 3:
                        if new:
                            tokens_T(f)
                    if s == 5:
                        if new:
                            gate(f, 1)
                    if s == 6:
                        if k == 0:
                            weight_T(4)
                        if old:
                            down(p, 1)
                    if s == 7:
                        if k == 0:
                            weight_T(5)
                    if g + AHEAD < B * STEPS:
                        B_rows(g + AHEAD)
                    if s == 1:
                        if k == 0:
                            x_dbl(1)
                            gate_T(0)
                        if k >= 1:
                            gate_T(k)
                    if s == 2:
                        if old:
                            q2_T(p, 0)
                            hadamard_mm(p, 1)
                    if s == 4:
                        if new:
                            gate(f, 0)
                    if s == 5:
                        if new:
                            up(f, 0)
                        if k == 0:
                            weight_T(2)
                    if s == 6:
                        if new:
                            up(f, 1)
                    if g + 1 < B * STEPS:
                        C_rows(g + 1)
                    accumulate(g)
                    if s == 0:
                        if old:
                            hadamard_mm(p, 0)
                    if s == 2:
                        if old:
                            down(p, 0)
                        if k == 0:
                            dt_proj(1)
                    if s == 3:
                        if front:
                            in_proj(n)
                        if k == 0:
                            weight_T(0)
                    if s == 4:
                        if k == 0:
                            weight_T(1)
                        if old:
                            q2_T(p, 1)
                    if s == 5:
                        if k == 0:
                            weight_T(3)
                        if front:
                            x_dbl(n)
                    if s == 7:
                        if front:
                            dt_proj(n)
                        if new:
                            inter_T(f, 0)
            p, f = B - 2, B - 1
            hadamard_mm(p, 0)
            inter_T(p, 1)
            tokens_T(f)
            hadamard_mm(p, 1)
            gate(f, 0)
            q2_T(p, 0)
            gate(f, 1)
            up(f, 0)
            up(f, 1)
            down(p, 0)
            inter_T(f, 0)
            hadamard_mm(f, 0)
            q2_T(p, 1)
            inter_T(f, 1)
            down(p, 1)
            hadamard_mm(f, 1)
            q2_T(f, 0)
            q2_T(f, 1)
            down(f, 0)
            down(f, 1)

        @block.scalar
        def _(act):
            def setup_loads():
                act.dma_start(id32[:], ident).then_inc(ld_consts, 16)
                act.dma_start(cw[:], conv_w.rearrange("(h p) k -> p h k", p=P)).then_inc(ld_taps, 16)
                act.dma_start(gates[:, 0:1], g_xattn.partition_broadcast(P)).then_inc(ld_gate, 16)
                act.dma_start(gates[:, 1:2], g_ffn.partition_broadcast(P)).then_inc(ld_gate, 16)
                act.dma_start(alog[:], A_log.rearrange("(h p) n -> p h n", p=P)).then_inc(ld_gate, 16)

            def copy_B(m):
                act.wait_ge(pe_B, m + 1)
                if RING <= m < RING + DVE_DRIVES:
                    act.wait_ge(dve_drive, m - RING + 1)
                elif m >= RING:
                    act.wait_ge(pool_drive, drives_before(m - RING + 1))
                nc.scalar.copy(Bs[:, m % RING], PB.rearrange("p (n l) -> p n l", n=NB)).then_inc(act_B, 1)

            def decays(m):
                b, j = divmod(m, STEPS)
                act.wait_ge(delta_ready, b + 1)
                if m >= RING:
                    act.wait_ge(dve_scan, m - RING + 1)
                for h in range(HALF):
                    for n in range(NB):
                        last = nc.scalar.activation(decay[:, m % RING, h, n, 1:L], delta[:, b % 2, h, 1:L], ACT.Exp,
                                                    bias=zero_c[:], scale=aneg[:, h, NB * j + n:NB * j + n + 1])
                last.then_inc(act_decay, 1)

            def conv_out(n):
                act.wait_ge(pe_xin, n + 1)
                act.wait_ge(act_u, n)
                for h in range(HALF):
                    last = nc.scalar.activation(conv[:, h, :], X[:, L * h:L * (h + 1)], ACT.Identity, bias=cb[:, h:h + 1])
                last.then_inc(act_conv, 1)

            def silu_u(n):
                if n == 1:
                    act.wait_ge(pe_xin, n + 1)
                    for h in range(HALF):
                        last = nc.scalar.activation(u[:, n, h], bank4[:, L * h:L * (h + 1)], ACT.Silu, bias=cb[:, h:h + 1])
                    last.then_inc(act_u, 1)
                else:
                    act.wait_ge(act_conv, n - 1)
                    if n >= 3:
                        act.wait_ge(du_ready, n - 2)
                        act.wait_ge(pe_y, n - 2)
                    nc.scalar.activation(u[:, n % 3], conv[:], ACT.Silu, bias=zero_c[:]).then_inc(act_u, 1)

            def silu_z(n):
                act.wait_ge(pool_zn, n + 1)
                if n >= 1:
                    act.wait_ge(pe_szT, n)
                nc.scalar.activation(sz[:], zn[:], ACT.Silu, bias=zero_c[:]).then_inc(act_sz, 1)

            def high_pieces(n):
                act.wait_ge(pe_xdbl, n + 1)
                if n >= 1:
                    act.wait_ge(dve_split, n)
                nc.scalar.copy(high[:], front_bank(n)[0:2 * 2 * DS, 0:L]).then_inc(act_high, 1)
                nc.scalar.copy(bc3[4 * DS:6 * DS, n], front_bank(n)[4 * DS:6 * DS, 0:L]).then_inc(act_high0, 1)

            def dt_rows(n):
                act.wait_ge(pe_xdbl, n + 1)
                nc.scalar.copy(dtlo[DT0:DT0 + DR, :], front_bank(n)[DT0:DT0 + DR, 0:L]).then_inc(act_dtlo, 1)

            def softplus(n):
                link = act_sp_link.begin(act, n)
                act.wait_ge(pe_draw, n + 1)
                if n >= 1:
                    act.wait_ge(delta_ready, n)
                for h in range(HALF):
                    v = dt_bank(n)[:, L * h:L * (h + 1)]
                    nc.scalar.activation(spr[:, h], v, ACT.Relu, bias=dtb[:, h:h + 1])
                    last = nc.scalar.activation(spa[:, h], v, ACT.Abs, bias=dtb[:, h:h + 1])
                last.then_inc(act_spread, 1)
                act.wait_ge(act_spread, n + 1)
                link(nc.scalar.activation(spe[:], spa[:], ACT.Exp, bias=zero_c[:], scale=-1.0))
                nc.scalar.activation(spl[:], spe[:], ACT.Ln, bias=one_c[:]).then_inc(act_sp, 1)
                link.end()

            def gate_out(k):
                act.wait_ge(pe_szT, k + 1)
                if k >= 1:
                    act.wait_ge(dve_x2, k)
                nc.scalar.activation(szT[:], (bank5 if k == 0 else X).rearrange("p (c e) -> p c e", c=LC), ACT.Copy,
                                     scale=tg[:, 0:1]).then_inc(act_szT, 1)

            def rstd2(f):
                link = act_r2_link.begin(act, f)
                act.wait_ge(dve_stat2, f + 1)
                link(nc.scalar.activation(ln2[:], mv2[:, :, 1], ACT.Ln, bias=eps_c[:]))
                nc.scalar.activation(r2[:], ln2[:], ACT.Exp, bias=zero_c[:], scale=-0.5).then_inc(act_r2, 1)
                link.end()

            def second_norm(f):
                act.wait_ge(dve_r2, f + 1)
                for c in range(LC):
                    last = nc.scalar.activation(xn[:, c], x2[:, f % 2, c], ACT.Identity, bias=mr2[:, c:c + 1],
                                                scale=r2[:, c:c + 1])
                last.then_inc(act_xn, 1)

            def scale_tokens(f):
                act.wait_ge(dve_ainv, f + 1)
                for c in range(LC):
                    last = nc.scalar.activation(xn[:, c], xn[:, c], ACT.Identity, bias=magic_c[:], scale=ainv[:, c:c + 1])
                last.then_inc(act_xr, 1)

            def silu_gate(f, t):
                act.wait_ge(pe_gate, LC * f + t + 1)
                act.wait_ge(dve_gs, f + 1)
                nc.scalar.activation(sg[:, t], (GP, UP)[t][:], ACT.Silu, bias=zero_c[:], scale=gs[:, t:t + 1]).then_inc(act_sg, 1)

            def inter_out(f, t):
                act.wait_ge(pe_tp, LC * f + t + 1)
                nc.scalar.copy(hT[:, t].rearrange("p a c -> p (a c)"), GP[:]).then_inc(act_tp, 1)

            def quant_down(f, t):
                act.wait_ge(dve_sc, LC * f + t + 1)
                if LC * f + t >= 1:
                    act.wait_ge(dve_q2, LC * f + t)
                nc.scalar.activation(tq, transform_bank(f, t)[:], ACT.Identity, bias=magic_c[:], scale=sc2[:, t:t + 1]
                                     ).then_inc(act_tq, 1)

            def for_silu():
                nc.scalar.preload_act_table_set("silu_and_others")

            def for_exp():
                nc.scalar.preload_act_table_set("natural_log_exp_and_others")

            setup_loads()
            for_silu()
            act.wait_ge(consts, 1)
            act.wait_ge(ld_taps, 16)
            act.wait_ge(ld_conv, 16 * 3)
            act.wait_ge(pe_xin, 1)
            for h in range(HALF):
                last = nc.scalar.activation(conv[:, h], bank4[:, L * h:L * (h + 1)], ACT.Identity, bias=cb[:, h:h + 1],
                                            scale=cw[:, h, DC - 1:DC])
            last.then_inc(act_tap, 1)
            act.wait_ge(pe_setup, 3)
            xp = PY[:, 0:HALF * P].rearrange("p (h k) -> p h k", h=HALF)
            nc.scalar.copy(xpwT[:, :, 0:DT0].rearrange("p h (i k) -> p h i k", i=3),
                           xp[:, :, DR:DR + 2 * DS].unsqueeze(2).to_broadcast([P, HALF, 3, 2 * DS]))
            nc.scalar.copy(xpwT[:, :, DT0:DT0 + DR], xp[:, :, 0:DR]).then_inc(act_setup, 1)
            act.wait_ge(pe_setup, 4)
            nc.scalar.copy(dtwT[DT0:DT0 + DR, :], PB[DT0:DT0 + DR, 0:E]).then_inc(act_setup, 1)
            act.wait_ge(ld_gate, 16 * 3)
            nc.scalar.activation(tg[:], gates[:], ACT.Tanh, bias=zero_c[:]).then_inc(act_gate, 1)
            act.wait_ge(dve_conv, 2 * (DC - 1))
            nc.scalar.activation(u[:, 0], conv[:], ACT.Silu, bias=zero_c[:]).then_inc(act_u, 1)
            for_exp()
            nc.scalar.activation(aneg[:], alog[:], ACT.Exp, bias=zero_c[:]).then_inc(act_gate, 1)
            dt_rows(0)
            high_pieces(0)
            act.wait_ge(pe_setup, 5)
            nc.scalar.copy(inwT[:].rearrange("p k e -> p (k e)"), UP[:]).then_inc(act_setup, 1)
            softplus(0)
            copy_B(0)
            act.wait_ge(pe_setup, 6)
            nc.scalar.copy(ctxT[:, 1:3], PC.rearrange("p (b l) -> p b l", b=2))
            nc.scalar.copy(ctxT[:, 3], PY[:, 0:L]).then_inc(act_setup, 1)
            act.wait_ge(dve_stat1, 1)
            nc.scalar.activation(ln1[:], mv1[:, :, 1], ACT.Ln, bias=eps_c[:]).then_inc(act_r1, 1)
            act.wait_ge(act_r1, 1)
            nc.scalar.activation(r1[:], ln1[:], ACT.Exp, bias=zero_c[:], scale=-0.5).then_inc(act_r1, 1)
            act.wait_ge(dve_aneg, 1)
            act.wait_ge(decay_zeroed, 1)
            decays(0)
            for m in range(1, AHEAD):
                copy_B(m)
                decays(m)
            for k in range(B):
                p, f, n = k - 2, k - 1, k + 2
                old, new, front = p >= 0, f >= 0, n < B
                for s in range(STEPS):
                    g = STEPS * k + s
                    if s == 0:
                        if new:
                            rstd2(f)
                    if s == 1:
                        if k == 0:
                            high_pieces(1)
                        if new:
                            second_norm(f)
                    if s == 2:
                        if k == 0:
                            dt_rows(1)
                            gate_out(0)
                        if new:
                            scale_tokens(f)
                    if s == 3:
                        if old:
                            quant_down(p, 1)
                    if s == 7:
                        if front:
                            high_pieces(n)
                    if g + AHEAD < B * STEPS:
                        copy_B(g + AHEAD)
                        decays(g + AHEAD)
                    if s == 0:
                        if k == 0:
                            for_silu()
                            silu_u(1)
                            silu_z(0)
                            for_exp()
                    if s == 1:
                        if old:
                            quant_down(p, 0)
                            inter_out(p, 1)
                        if k >= 1:
                            gate_out(k)
                    if s == 3:
                        if k == 0:
                            softplus(1)
                        if front:
                            conv_out(n)
                    if s == 4:
                        if new or k + 1 < B:
                            for_silu()
                        if new:
                            silu_gate(f, 0)
                            silu_gate(f, 1)
                        if front:
                            silu_u(n)
                        if k + 1 < B:
                            silu_z(k + 1)
                        for_exp()
                    if s == 5:
                        if front:
                            dt_rows(n)
                    if s == 7:
                        if new:
                            inter_out(f, 0)
                        if front:
                            softplus(n)
            p, f = B - 2, B - 1
            rstd2(f)
            for_silu()
            second_norm(f)
            scale_tokens(f)
            inter_out(p, 1)
            quant_down(p, 0)
            silu_gate(f, 0)
            quant_down(p, 1)
            silu_gate(f, 1)
            inter_out(f, 0)
            inter_out(f, 1)
            quant_down(f, 0)
            quant_down(f, 1)

        @block.gpsimd
        def _(pool):
            def drives(m):
                b, j = divmod(m, STEPS)
                pool.wait_ge(act_B, m + 1)
                pool.wait_ge(du_ready, b + 1)
                if m >= RING:
                    pool.wait_ge(dve_scan, m - RING + 1)
                for h in range(HALF):
                    last = nc.gpsimd.tensor_tensor(
                        drive[:, m % RING, h], du[:, b % 2, h, :].unsqueeze(1).to_broadcast([P, NB, L]),
                        Bs[:, m % RING], ALU.mult)
                last.then_inc(pool_drive, 1)

            def norm_z(n):
                pool.wait_ge(dve_r1, 1)
                if n >= 1:
                    pool.wait_ge(act_sz, n)
                for h in range(HALF):
                    i = HALF * n + h
                    last = nc.gpsimd.tensor_scalar(zn[:, h], xs[:, n, h], r1[:, i:i + 1], mr1[:, i:i + 1],
                                                   ALU.mult, ALU.add)
                last.then_inc(pool_zn, 1)

            def fold_tile(f, t, stage):
                if stage == 0:
                    pool.wait_ge(dve_mul, LC * f + t + 1)
                    src, dst, done, gap = inter, fold, pool_stage, 4
                else:
                    pool.wait_ge(pool_stage, LC * f + t + 1)
                    src, dst, done, gap = fold, inter, pool_fold, 2
                src, dst = (v[:, t].rearrange("p (g s w) -> p g s w", s=2, w=gap * P) for v in (src, dst))
                nc.gpsimd.tensor_tensor(dst[:, :, 0, :], src[:, :, 0, :], src[:, :, 1, :], ALU.add)
                nc.gpsimd.tensor_tensor(dst[:, :, 1, :], src[:, :, 0, :], src[:, :, 1, :], ALU.subtract).then_inc(done, 1)

            def weight_scale(m):
                pool.wait_ge(dve_winv, 1)
                pool.wait_ge(ld_w[m], 16)
                nc.gpsimd.tensor_scalar(wnat[:, m], wnat[:, m], winv[:, m:m + 1], MAGIC, ALU.mult, ALU.add
                                        ).then_inc(pool_wt, 1)

            def build_hadamard():
                pool.wait_ge(ld_had, 16)
                pool.wait_ge(dve_wq, 3)
                v = had2.rearrange("p j i c -> p (j i) c")
                nc.gpsimd.tensor_copy(v[:, 0:3], had[:].unsqueeze(1).to_broadcast([P, 3, P]))
                nc.gpsimd.tensor_scalar(v[:, 3], had[:], -1.0, 1.0, ALU.mult, ALU.mult).then_inc(had_built, 1)

            nc.gpsimd.memset(dtw[:], 0.0).then_inc(zeroed, 1)
            nc.gpsimd.memset(zero_c[:], 0.0)
            nc.gpsimd.memset(one_c[:], 1.0)
            nc.gpsimd.memset(eps_c[:], LN_EPS)
            nc.gpsimd.memset(onesf[:], 1.0)
            nc.gpsimd.memset(magic_c[:], MAGIC).then_inc(consts, 1)
            for r in range(RING):
                last = nc.gpsimd.memset(decay[:, r, :, :, 0:1], 0.0)
            last.then_inc(decay_zeroed, 1)
            pool.wait_ge(ld_consts, 16)
            pool.wait_ge(ld_conv, 16 * 3)
            for h in range(HALF):
                last = nc.gpsimd.tensor_scalar(diag[:, h], id32[:], dskip[:, h:h + 1], 1.0, ALU.mult, ALU.mult)
            last.then_inc(pool_diag, 1)
            for m in range(DVE_DRIVES, AHEAD):
                drives(m)
            for k in range(B):
                p, f, n = k - 2, k - 1, k + 2
                old, new, front = p >= 0, f >= 0, n < B
                for s in range(STEPS):
                    g = STEPS * k + s
                    if s == 1:
                        if k == 0:
                            norm_z(0)
                    if s == 2:
                        if 1 <= k < B - 1:
                            softplus_tail(k + 1, pool, nc.gpsimd, pool_front_link, 1)
                    if s == 3:
                        if 1 <= k < B - 1:
                            softplus_tail(k + 1, pool, nc.gpsimd, pool_front_link, 2)
                    if s == 6:
                        if new:
                            fold_tile(f, 1, 0)
                    if g + AHEAD < B * STEPS:
                        drives(g + AHEAD)
                    if s == 1:
                        if k == 0:
                            weight_scale(0)
                        if 1 <= k < B - 1:
                            pool_front_link.begin(pool, k + 1 - 2)
                            softplus_tail(k + 1, pool, nc.gpsimd, pool_front_link, 0)
                    if s == 2:
                        if k + 1 < B:
                            norm_z(k + 1)
                        if k == 0:
                            weight_scale(1)
                    if s == 4:
                        if new:
                            fold_tile(f, 0, 0)
                        if k == 0:
                            weight_scale(2)
                    if s == 5:
                        if new:
                            fold_tile(f, 0, 1)
                        if k == 0:
                            build_hadamard()
                    if s == 7:
                        if new:
                            fold_tile(f, 1, 1)
            p, f = B - 2, B - 1
            fold_last(0, pool, nc.gpsimd, slice(DVE_COLS, P), pool_fold_last)
            fold_last(1, pool, nc.gpsimd, slice(DVE_COLS, P), pool_fold_last)

        @block.vector
        def _(dve):
            once = [0]

            def link_once(ins):
                once[0] += 1
                ins.then_inc(dve_once, 1)
                dve.wait_ge(dve_once, once[0])

            def newton(link, r, v, tmp):
                link(nc.vector.scalar_tensor_tensor(out=tmp, in0=r, scalar=-0.5, in1=v, op0=ALU.mult, op1=ALU.mult))
                link(nc.vector.tensor_tensor(tmp, tmp, r, ALU.mult))
                return nc.vector.scalar_tensor_tensor(out=r, in0=tmp, scalar=1.5, in1=r, op0=ALU.add, op1=ALU.mult)

            def scan(g):
                dve.wait_ge(act_decay, g + 1)
                if g < DVE_DRIVES:
                    dve.wait_ge(dve_drive, g + 1)
                else:
                    dve.wait_ge(pool_drive, drives_before(g + 1))
                if g >= STATES:
                    dve.wait_ge(dve_prod, g - STATES + 1)
                nc.vector.tensor_tensor_scan(
                    state[:, g % STATES].rearrange("p h n l -> p (h n l)"), decay[:, g % RING].rearrange("p h n l -> p (h n l)"),
                    drive[:, g % RING].rearrange("p h n l -> p (h n l)"), 0.0, ALU.mult, ALU.add).then_inc(dve_scan, 1)

            def first_conv():
                for d in range(1, DC):
                    for h in range(HALF):
                        if d == 1:
                            dve.wait_ge(act_tap, 1)
                        else:
                            dve.wait_ge(dve_conv, HALF * (d - 2) + h + 1)
                        nc.vector.scalar_tensor_tensor(out=conv[:, h, d:L], in0=bank4[:, L * h:L * (h + 1) - d],
                                                       scalar=cw[:, h, DC - 1 - d:DC - d], in1=conv[:, h, d:L],
                                                       op0=ALU.mult, op1=ALU.add).then_inc(dve_conv, 1)

            def delta_on_vector(n):
                link = dve_front_link.begin(dve, n)
                dve.wait_ge(act_sp, n + 1)
                link(nc.vector.tensor_scalar(spm[:], spe[:], 1.0, None, ALU.add))
                link(nc.vector.scalar_tensor_tensor(out=spm[:], in0=spm[:], scalar=-1.0, in1=spe[:],
                                                    op0=ALU.add, op1=ALU.subtract))
                link(nc.vector.tensor_tensor(spl[:], spl[:], spm[:], ALU.subtract))
                nc.vector.tensor_tensor(delta[:, n], spl[:], spr[:], ALU.add).then_inc(delta_ready, 1)
                du_of(n, dve, nc.vector)
                link.end()

            def first_drive(m):
                dve.wait_ge(act_B, m + 1)
                dve.wait_ge(du_ready, 1)
                for h in range(HALF):
                    last = nc.vector.tensor_tensor(drive[:, m, h], du[:, 0, h, :].unsqueeze(1).to_broadcast([P, NB, L]),
                                                   Bs[:, m], ALU.mult)
                last.then_inc(dve_drive, 1)

            def times_C(g):
                dve.wait_ge(dve_scan, g + 1)
                dve.wait_ge(pe_C, g + 1)
                if g >= RING:
                    dve.wait_ge(pe_acc, g - RING + 1)
                nc.vector.tensor_tensor(
                    prod[:, g % RING].rearrange("p h n l -> p h (n l)"),
                    state[:, g % STATES].rearrange("p h n l -> p h (n l)"),
                    PC.unsqueeze(1).to_broadcast([P, HALF, NB * L]), ALU.mult).then_inc(dve_prod, 1)

            def split(n):
                link = dve_split_link.begin(dve, n)
                k = 2 * DS
                dve.wait_ge(act_high, n + 1)
                src = front_bank(n)
                nc.vector.tensor_tensor(bc3[0:2 * k, n], src[0:2 * k, 0:L], high[:], ALU.subtract)
                link(nc.vector.tensor_tensor(rest[k:2 * k], src[k:2 * k, 0:L], high[k:2 * k], ALU.subtract))
                nc.vector.tensor_tensor(bc3[k:2 * k, n], rest[k:2 * k], bc3[k:2 * k, n], ALU.subtract
                                        ).then_inc(dve_split, 1)
                link.end()

            def residual(f):
                dve.wait_ge(pe_y, f + 1)
                dve.wait_ge(act_szT, f + 1)
                nc.vector.tensor_tensor(yg[:], PY[:].rearrange("p (c e) -> p c e", c=LC), szT[:],
                                        ALU.mult).then_inc(dve_x2, 1)

            def stats2(f, link):
                dve.wait_ge(dve_x2, f + 1)
                link(nc.vector.tensor_tensor(x2[:, f % 2], yg[:], xs[:, f], ALU.add))
                for c in range(LC):
                    ins = nc.vector.bn_stats(st2[:, c], x2[:, f % 2, c])
                link(ins)
                for c in range(LC):
                    ins = nc.vector.bn_aggr(mv2[:, c], st2[:, c])
                ins.then_inc(dve_stat2, 1)

            def second_rstd(f, link):
                dve.wait_ge(dve_stat2, f + 1)
                link(nc.vector.tensor_scalar(ve2[:], mv2[:, :, 1], LN_EPS, None, ALU.add))
                dve.wait_ge(act_r2, f + 1)
                link(newton(link, r2[:], ve2[:], nt2[:]))
                nc.vector.scalar_tensor_tensor(out=mr2[:], in0=mv2[:, :, 0], scalar=-1.0, in1=r2[:],
                                               op0=ALU.mult, op1=ALU.mult).then_inc(dve_r2, 1)

            def token_scale(f, link):
                dve.wait_ge(act_xn, f + 1)
                link(nc.vector.tensor_reduce(amax[:], xn[:], AX.X, ALU.max, apply_absolute_value=True))
                link(nc.vector.tensor_scalar(amax[:], amax[:], Q_EPS, 1.0 / QB, ALU.max, ALU.mult))
                nc.vector.reciprocal(ainv[:], amax[:]).then_inc(dve_ainv, 1)
                nc.vector.tensor_scalar(gs[:], amax[:], wmean[:, 0:1], None, ALU.mult)
                nc.vector.tensor_scalar(us[:], amax[:], wmean[:, 1:2], None, ALU.mult).then_inc(dve_gs, 1)
                link.end()

            def round_tokens(f):
                dve.wait_ge(act_xr, f + 1)
                nc.vector.tensor_scalar(q[:], xn[:], MAGIC + QB - 1, MAGIC, ALU.min, ALU.subtract).then_inc(dve_q, 1)

            def tokens_out(f):
                dve.wait_ge(pe_qT, f + 1)
                nc.vector.tensor_scalar(qT[:], X.bitcast(BF16)[:, 0:HALF * L].rearrange("p (h l) -> p h l", h=HALF),
                                        -QB, None, ALU.max).then_inc(dve_qT, 1)

            def gate_times_up(f, t):
                dve.wait_ge(act_sg, LC * f + t + 1)
                dve.wait_ge(pe_up, LC * f + t + 1)
                dve.wait_ge(dve_gs, f + 1)
                nc.vector.scalar_tensor_tensor(out=inter[:, t], in0=(GP, UP)[t][:], scalar=us[:, t:t + 1], in1=sg[:, t],
                                               op0=ALU.mult, op1=ALU.mult).then_inc(dve_mul, 1)

            def absmax2(f, t):
                link = dve_sc_link.begin(dve, LC * f + t)
                dve.wait_ge(pe_h, LC * f + t + 1)
                a = am2[:, t:t + 1]
                link(nc.vector.tensor_reduce(a, transform_bank(f, t)[:], AX.X, ALU.max, apply_absolute_value=True))
                link(nc.vector.tensor_scalar(a, a, Q_EPS, 1.0 / QB, ALU.max, ALU.mult))
                nc.vector.reciprocal(sc2[:, t:t + 1], a).then_inc(dve_sc, 1)
                nc.vector.tensor_scalar(dq2[:, t:t + 1], a, wdn[:], None, ALU.mult).then_inc(dve_dq, 1)
                link.end()

            def round_down(f, t):
                dve.wait_ge(act_tq, LC * f + t + 1)
                nc.vector.tensor_scalar(q2[:, t], tq, MAGIC + QB - 1, MAGIC, ALU.min, ALU.subtract).then_inc(dve_q2, 1)

            def q2_out(f, t):
                dve.wait_ge(pe_q2T, LC * f + t + 1)
                nc.vector.tensor_scalar(q2T[:, t], q2_bank(f, t).bitcast(BF16).rearrange("p (a c) -> p a c", a=NI),
                                        -QB, None, ALU.max).then_inc(dve_q2T, 1)

            def result(f, t):
                dve.wait_ge(pe_dn, LC * f + t + 1)
                dve.wait_ge(dve_dq, LC * f + t + 1)
                if f >= 1:
                    dve.wait_ge(stored[t], 16 * f)
                nc.vector.scalar_tensor_tensor(out=ot[:, t], in0=down_bank(f, t)[:, 0:E], scalar=dq2[:, t:t + 1],
                                               in1=x2[:, f % 2, t], op0=ALU.mult, op1=ALU.add).then_inc(dve_out, 1)

            def weight_abs(m):
                dve.wait_ge(ld_w[m], 16)
                nc.vector.tensor_reduce(wsum[:, m:m + 1], wnat[:, m], AX.X, ALU.add,
                                        apply_absolute_value=True).then_inc(wabs_done, 1)

            def weight_means():
                dve.wait_ge(pe_wsum, 1)
                dve.wait_ge(act_gate, 1)
                link_once(nc.vector.tensor_scalar(wmean[:], bank7[:, 0:3], 1.0 / (2 * P * I), Q_EPS, ALU.mult, ALU.max))
                nc.vector.tensor_tensor(wdn[:], wmean[:, 2:3], tg[:, 1:2], ALU.mult)
                nc.vector.reciprocal(winv[:], wmean[:]).then_inc(dve_winv, 1)

            def weight_round(m):
                dve.wait_ge(pool_wt, m + 1)
                nc.vector.tensor_scalar(wq[:, m], wnat[:, m], MAGIC + 1.0, MAGIC, ALU.min, ALU.subtract).then_inc(dve_wq, 1)

            def weight_out(i):
                dve.wait_ge(pe_wT, i + 1)
                nc.vector.tensor_scalar(wT[:].rearrange("p m n -> p (m n)")[:, I * i:I * (i + 1)],
                                        (bank7 if i % 2 == 0 else bank6).bitcast(BF16), -1.0, None, ALU.max
                                        ).then_inc(dve_wT, 1)

            def first_norm():
                dve.wait_ge(ld_x, 16)
                for i in range(B * LC):
                    last = nc.vector.bn_stats(st1[:, i], xs[:, i // LC, i % LC])
                link_once(last)
                for i in range(B * LC):
                    last = nc.vector.bn_aggr(mv1[:, i], st1[:, i])
                last.then_inc(dve_stat1, 1)
                dve.wait_ge(dve_stat1, 1)
                link_once(nc.vector.tensor_scalar(ve1[:], mv1[:, :, 1], LN_EPS, None, ALU.add))

            dve.wait_ge(ld_consts, 16)
            nc.vector.tensor_copy(id16[:], id32[:])
            for i in range(3):
                k = slice(2 * DS * i, 2 * DS * (i + 1))
                last = nc.vector.tensor_copy(sel[k, :], id32[k, k])
            last.then_inc(dve_consts, 1)
            dve.wait_ge(pe_setup, 1)
            nc.vector.tensor_copy(ctxT[:, 0], bank4[:, 0:L]).then_inc(dve_setup, 1)
            dve.wait_ge(pe_setup, 2)
            nc.vector.tensor_copy(inw0T, bank5[:, 0:E]).then_inc(dve_setup, 1)
            dve.wait_ge(ld_inw, 16)
            dve.wait_ge(ld_taps, 16)
            for k in range(DC):
                for h in range(HALF):
                    last = nc.vector.tensor_scalar(inwk[:, k, h], inw[:, h], cw[:, h, k:k + 1], None, ALU.mult)
                if k % 2 == 1:
                    last.then_inc(dve_inwk, 1)
            first_conv()
            weight_abs(0)
            split(0)
            dve.wait_ge(act_gate, 2)
            nc.vector.tensor_scalar(aneg[:], aneg[:], -1.0, None, ALU.mult).then_inc(dve_aneg, 1)
            first_norm()
            delta_on_vector(0)
            first_drive(0)
            scan(0)
            first_drive(1)
            dve.wait_ge(act_r1, 2)
            link_once(newton(link_once, r1[:], ve1[:], nt1[:]))
            nc.vector.scalar_tensor_tensor(out=mr1[:], in0=mv1[:, :, 0], scalar=-1.0, in1=r1[:],
                                           op0=ALU.mult, op1=ALU.mult).then_inc(dve_r1, 1)
            weight_abs(1)
            for k in range(B):
                p, f, n = k - 2, k - 1, k + 2
                old, new, front = p >= 0, f >= 0, n < B
                for s in range(STEPS):
                    g = STEPS * k + s
                    if s == 1:
                        if new:
                            stats2(f, dve_ln_link.begin(dve, f))
                    if s == 3:
                        if k == 0:
                            split(1)
                    if s == 4:
                        if old:
                            round_down(p, 1)
                    if s == 6:
                        if old:
                            q2_out(p, 1)
                    if g + 1 < B * STEPS:
                        scan(g + 1)
                    if s == 0:
                        if 1 <= k < B - 1:
                            split(k + 1)
                    if s == 1:
                        if new:
                            second_rstd(f, dve_ln_link)
                    if s == 2:
                        if old:
                            round_down(p, 0)
                        if new:
                            token_scale(f, dve_ln_link)
                    if s == 3:
                        if k == 0:
                            weight_means()
                        if new:
                            round_tokens(f)
                        if old:
                            q2_out(p, 0)
                            absmax2(p, 1)
                    if s == 4:
                        if old:
                            result(p, 0)
                    if s == 5:
                        if k == 0:
                            weight_out(0)
                            delta_on_vector(1)
                            weight_round(1)
                    if s == 6:
                        if new:
                            gate_times_up(f, 0)
                    if s == 7:
                        if k == 0:
                            weight_out(3)
                        if old:
                            result(p, 1)
                        if new:
                            gate_times_up(f, 1)
                        if k == 0:
                            weight_out(5)
                    times_C(g)
                    if s == 0:
                        if new:
                            residual(f)
                        if k == 0:
                            weight_abs(2)
                    if s == 1:
                        if old:
                            absmax2(p, 0)
                    if s == 3:
                        if new:
                            tokens_out(f)
                    if s == 4:
                        if k == 0:
                            weight_round(0)
                    if s == 5:
                        if k == 0:
                            weight_out(1)
                    if s == 6:
                        if k == 0:
                            weight_round(2)
                            weight_out(2)
                    if s == 7:
                        if k == 0:
                            weight_out(4)
            p, f = B - 2, B - 1
            residual(f)
            stats2(f, dve_ln_link.begin(dve, f))
            second_rstd(f, dve_ln_link)
            token_scale(f, dve_ln_link)
            round_tokens(f)
            absmax2(p, 0)
            round_down(p, 0)
            tokens_out(f)
            absmax2(p, 1)
            q2_out(p, 0)
            gate_times_up(f, 0)
            fold_last(0, dve, nc.vector, slice(0, DVE_COLS), dve_fold)
            gate_times_up(f, 1)
            result(p, 0)
            round_down(p, 1)
            fold_last(1, dve, nc.vector, slice(0, DVE_COLS), dve_fold)
            q2_out(p, 1)
            absmax2(f, 0)
            result(p, 1)
            round_down(f, 0)
            absmax2(f, 1)
            q2_out(f, 0)
            round_down(f, 1)
            q2_out(f, 1)
            result(f, 0)
            result(f, 1)


def tiles(t):
    return t.rearrange("b l n -> (b l) n").rearrange("(c p) n -> p c n", p=P)


_INS = ['x', 'ctx_1024', 'g_xattn', 'g_ffn', 'L0_xattn_in_proj_w', 'L0_xattn_conv_w', 'L0_xattn_conv_b',
        'L0_xattn_x_proj_w', 'L0_xattn_dt_proj_w', 'L0_xattn_dt_proj_b', 'L0_xattn_A_log', 'L0_xattn_D',
        'L0_ffn_w_gate', 'L0_ffn_w_up', 'L0_ffn_w_down']


def _constants():
    import numpy as np
    h = np.ones((1, 1), np.float32)
    while h.shape[0] < P:
        h = np.block([[h, h], [h, -h]])
    return {"ident": np.eye(P, dtype=np.float32), "hadamard": (h / math.sqrt(I)).astype(np.float32)}


def kernel(**inputs):
    import numpy as np
    import concourse.bacc as bacc
    from concourse.bass_utils import run_bass_kernel_spmd

    nc = bacc.Bacc("TRN2", target_bir_lowering=False, num_devices=1)
    arrays, args = {}, []
    for name, a in [(n, np.ascontiguousarray(inputs[n])) for n in _INS] + list(_constants().items()):
        arrays[f"in_{name}_dram"] = a
        args.append(nc.dram_tensor(f"in_{name}_dram", a.shape, mybir.dt.from_np(a.dtype), kind="ExternalInput").ap())
    out = nc.dram_tensor("out_0_dram", (B, L, E), F32, kind="ExternalOutput").ap()
    gated_ssm_ffn(nc, *args, out)
    return run_bass_kernel_spmd(nc, [arrays], core_ids=[0]).results[0]["out_0_dram"]
```
